# Optimizing a Trainium2 kernel written in Bass

```python
import numpy as np
import jax
import jax.numpy as jnp

def _softmax(x, axis=-1):
    return jax.nn.softmax(x, axis=axis)

def _gelu(x):
    return jax.nn.gelu(x, approximate=True)

def _silu(x):
    return jax.nn.silu(x)

def _sigmoid(x):
    return jax.nn.sigmoid(x)

def _layernorm(x, axis=-1, eps=1e-05):
    m = jnp.mean(x, axis=axis, keepdims=True)
    v = jnp.var(x, axis=axis, keepdims=True)
    return (x - m) / jnp.sqrt(v + eps)

def _scatter_add(tgt, idx, src, axis=0):
    return tgt.at[idx].add(src)

def _segment_sum(src, seg, n):
    return jax.ops.segment_sum(src, seg, n)
kernel_name = 'mk_adaln_d1_jaxref_r8_2db6c0'

def setup_inputs(seed: int=0):
    np.random.seed(seed)
    _w = jnp.asarray

    def _L0_attn_setup():
        import jax, jax.numpy as jnp
        import numpy as np
        BH = 32
        BW = 32
        key = jax.random.key(seed)
        k1, k2, k3, k4 = jax.random.split(key, 4)
        B, S, K, N = (2, 256, 512, 512)
        data = jax.random.normal(k1, (B, S, K), dtype=jnp.float32)
        weight = jax.random.normal(k2, (N, K), dtype=jnp.float32) * 0.02
        bias = jax.random.normal(k3, (N,), dtype=jnp.float32) * 0.02
        Nb, Kb = (N // BH, K // BW)
        block_on = jax.random.uniform(k4, (Nb, Kb)) < 0.3
        mask = jnp.repeat(jnp.repeat(block_on, BH, axis=0), BW, axis=1).astype(jnp.int32)
        return {'data': data, 'mask': mask, 'weight': weight, 'bias': bias}
    _L0_attn_in = _L0_attn_setup()

    def _L0_ffn_setup():
        import jax, jax.numpy as jnp
        import numpy as np
        DIM = 512
        HID = 1376
        R = 16
        SCALING = 32.0 / 16.0

        def _lora_linear(x, w, a, b):
            base = jnp.einsum('bsd,od->bso', x, w)
            low = jnp.einsum('bsr,or->bso', jnp.einsum('bsd,rd->bsr', x, a), b)
            return base + low * SCALING
        key = jax.random.key(seed)
        ks = jax.random.split(key, 10)
        s_in = 1.0 / np.sqrt(DIM)
        s_hid = 1.0 / np.sqrt(HID)
        return {'x': jax.random.normal(ks[0], (4, 256, DIM), jnp.float32), 'w1': jax.random.normal(ks[1], (HID, DIM), jnp.float32) * s_in, 'w3': jax.random.normal(ks[2], (HID, DIM), jnp.float32) * s_in, 'w2': jax.random.normal(ks[3], (DIM, HID), jnp.float32) * s_hid, 'lora_A1': jax.random.normal(ks[4], (R, DIM), jnp.float32) * s_in, 'lora_B1': jax.random.normal(ks[5], (HID, R), jnp.float32) * 0.02, 'lora_A3': jax.random.normal(ks[6], (R, DIM), jnp.float32) * s_in, 'lora_B3': jax.random.normal(ks[7], (HID, R), jnp.float32) * 0.02, 'lora_A2': jax.random.normal(ks[8], (R, HID), jnp.float32) * s_hid, 'lora_B2': jax.random.normal(ks[9], (DIM, R), jnp.float32) * 0.02}
    _L0_ffn_in = _L0_ffn_setup()
    _L0_c = _w((lambda *s: np.random.randn(*s).astype(np.float32) * 0.05)(2, 512))
    _L0_wmod = _w((lambda *s: np.random.randn(*s).astype(np.float32) * 0.05)(512, 6 * 512) * 512 ** (-0.5))
    _d = {'L0_attn_data': _L0_attn_in['data'], 'L0_attn_mask': _L0_attn_in['mask'], 'L0_attn_weight': _L0_attn_in['weight'], 'L0_attn_bias': _L0_attn_in['bias'], 'L0_ffn_w1': _L0_ffn_in['w1'], 'L0_ffn_w3': _L0_ffn_in['w3'], 'L0_ffn_w2': _L0_ffn_in['w2'], 'L0_ffn_lora_A1': _L0_ffn_in['lora_A1'], 'L0_ffn_lora_B1': _L0_ffn_in['lora_B1'], 'L0_ffn_lora_A3': _L0_ffn_in['lora_A3'], 'L0_ffn_lora_B3': _L0_ffn_in['lora_B3'], 'L0_ffn_lora_A2': _L0_ffn_in['lora_A2'], 'L0_ffn_lora_B2': _L0_ffn_in['lora_B2'], 'L0_c': _L0_c, 'L0_wmod': _L0_wmod}
    _x0 = _d['L0_attn_data']
    _d['L0_attn_data'] = jax.random.normal(jax.random.fold_in(jax.random.key(seed), 1), (2, 512, 512), dtype=_x0.dtype)
    del _x0
    return _d

def reference(L0_attn_data, L0_attn_mask, L0_attn_weight, L0_attn_bias, L0_ffn_w1, L0_ffn_w3, L0_ffn_w2, L0_ffn_lora_A1, L0_ffn_lora_B1, L0_ffn_lora_A3, L0_ffn_lora_B3, L0_ffn_lora_A2, L0_ffn_lora_B2, L0_c, L0_wmod):

    def _L0_attn_ref(data, mask, weight, bias):
        import jax, jax.numpy as jnp
        import numpy as np
        BH = 32
        BW = 32
        N, K = weight.shape
        Nb, Kb = (N // BH, K // BW)
        bm = mask.reshape(Nb, BH, Kb, BW).sum(axis=(1, 3)) > 0
        wb = weight.reshape(Nb, BH, Kb, BW) * bm[:, None, :, None].astype(weight.dtype)
        w = wb.reshape(N, K)
        out = jnp.einsum('bsk,nk->bsn', data, w) + bias
        return out

    def _L0_ffn_ref(x, w1, w3, w2, lora_A1, lora_B1, lora_A3, lora_B3, lora_A2, lora_B2):
        import jax, jax.numpy as jnp
        import numpy as np
        DIM = 512
        HID = 1376
        R = 16
        SCALING = 32.0 / 16.0

        def _lora_linear(x, w, a, b):
            base = jnp.einsum('bsd,od->bso', x, w)
            low = jnp.einsum('bsr,or->bso', jnp.einsum('bsd,rd->bsr', x, a), b)
            return base + low * SCALING
        h1 = _lora_linear(x, w1, lora_A1, lora_B1)
        h3 = _lora_linear(x, w3, lora_A3, lora_B3)
        g = jax.nn.silu(h1) * h3
        return _lora_linear(g, w2, lora_A2, lora_B2)
    x = L0_attn_data
    mod = (_silu(L0_c) @ L0_wmod).reshape(L0_c.shape[0], 6, 1, -1)
    sa, ca, ga, sb, cb, gb = (mod[:, 0], mod[:, 1], mod[:, 2], mod[:, 3], mod[:, 4], mod[:, 5])
    ga = (2 * (ga >= 0) - 1) * jnp.maximum(jnp.abs(ga), 0.25)
    gb = (2 * (gb >= 0) - 1) * jnp.maximum(jnp.abs(gb), 0.25)
    h = _layernorm(x, axis=-1) * (1 + ca) + sa
    x = x + ga * _L0_attn_ref(h, L0_attn_mask, L0_attn_weight, L0_attn_bias)
    h = _layernorm(x, axis=-1) * (1 + cb) + sb
    x = x + gb * _L0_ffn_ref(h, L0_ffn_w1, L0_ffn_w3, L0_ffn_w2, L0_ffn_lora_A1, L0_ffn_lora_B1, L0_ffn_lora_A3, L0_ffn_lora_B3, L0_ffn_lora_A2, L0_ffn_lora_B2)
    return x

_drawn_inputs = setup_inputs


def setup_inputs(seed=0):
    import zlib

    import numpy as np

    out = dict(_drawn_inputs(seed))
    spreads = {}
    factors = {'L0_attn_bias': 8.0}
    for name, (base, spread) in spreads.items():
        noise = np.random.default_rng([zlib.crc32(name.encode()), seed]).standard_normal(out[name].shape)
        drawn = base * np.exp(spread * noise) if base else spread * noise
        out[name] = jnp.asarray(drawn.astype(out[name].dtype))
    for name, factor in factors.items():
        out[name] = (out[name] * factor).astype(out[name].dtype)
    return out
```

```python
from contextlib import ExitStack

import numpy as np

import concourse.bass as bass
from concourse import mybir

P = 128
ALU = mybir.AluOpType
ACT = mybir.ActivationFunctionType
AX = mybir.AxisListType
F32 = mybir.dt.float32
F32R = mybir.dt.float32r
I32 = mybir.dt.int32

B, S, D, HID, R = 2, 512, 512, 1376, 16
BLOCK = 32
SCALING = 32.0 / 16.0
EPS = 1e-05
GATE_MIN = 0.25
KT = D // P
T = S // P
TILES = B * T
NORMS = 2 * TILES
HT = -(-HID // P)
WIDTH = [min(P, HID - j * P) for j in range(HT)]
NB = D // BLOCK
SLOTS = 5
WORK = 3
EARLY_TILES = 2
RANKS = 4 * R

SHIFT_A, SCALE_A, GATE_A, SHIFT_F, SCALE_F, GATE_F = (n * KT for n in range(6))

A2_COLS = -(-HT // 2) * P
LORA_B13, LORA_A13, LORA_A2, LORA_B2 = 0, HID, HID + D, HID + D + A2_COLS
LORA_COLS = LORA_B2 + D
LORA_CUTS = [(LORA_B13, LORA_A13), (LORA_A13, LORA_A2), (LORA_A2, LORA_B2), (LORA_B2, LORA_COLS)]

BLOCK_ONES, KEEP_B, KEEP_A, KEEP_BIAS = 0, P, P + 1, P + 2
CONST_COLS = P + 3

MERGES = [("merge", r) for r in range(3 * HT)]


def side_jobs():
    jobs = [("mask", 0), ("mod", 0), ("mod", 1), ("gate", 0), ("gate", 1)]
    jobs += [("norm", i) for i in (4, 5, 6, 7)] + [("mod", 2)]
    jobs += [("norm", 8), ("norm", 9), MERGES[0], ("norm", 10), MERGES[1], MERGES[2], ("norm", 11)]
    jobs += MERGES[3:6]
    for j in range(HT):
        jobs += MERGES[3 * (j + 2):3 * (j + 3)]
        if j < T:
            jobs.append(("norm", NORMS - T + j))
        elif j < T + B:
            jobs.append(("gate", B + j - T))
    return jobs


SIDE_JOBS = side_jobs()
SIDE = {job: n for n, job in enumerate(SIDE_JOBS)}
MOD_PARTS = [(SHIFT_A, 2 * KT), (GATE_A, KT), (SHIFT_F, 3 * KT)]


def build(nc, x, mask, weight, bias, ffn, lora, c, wmod, identity, consts, out):
    x_rows = x.rearrange("(b p t) d -> b p t d", b=B, p=P)
    out_rows = out.rearrange("b (p t) d -> b p t d", p=P)
    wmod_rows = wmod.rearrange("(k p) n -> p k n", p=P)

    with ExitStack() as ctx:
        def sb(name, shape, dt=F32, at=ctx):
            return at.enter_context(nc.sbuf_tensor(name, shape, dt))

        def sem(name):
            return ctx.enter_context(nc.semaphore(name))

        xt = sb("xt", [P, B, T, D])
        ht_hi = [sb(f"ht_hi{b}", [P, KT, S], F32R) for b in range(B)]
        ht_lo = [sb(f"ht_lo{b}", [P, KT, S], F32R) for b in range(B)]
        work = sb("work", [P, WORK, D])
        raw = sb("raw", [P, SLOTS, D])
        g = sb("g", [P, S])
        g_hi = [sb(f"g_hi{n}", [P, S], F32R) for n in range(2)]
        g_lo = [sb(f"g_lo{n}", [P, S], F32R) for n in range(2)]
        gate_row = sb("gate_row", [P, B, D])
        parts = sb("parts", [P, LORA_COLS], F32R)
        ident = sb("ident", [P, P])
        mod = sb("mod", [P, 6 * KT, B])
        one_plus = sb("one_plus", [P, 2 * KT, B])
        gates = sb("gates", [P, 2 * KT, B])
        gate_sign = sb("gate_sign", [P, KT, B])
        gate_size = sb("gate_size", [P, KT, B])
        stats = sb("stats", [P, 2, 6])
        moments = sb("moments", [P, NORMS, 2])
        var_eps = sb("var_eps", [P, NORMS])
        rstd = sb("rstd", [P, NORMS])
        minus_half = sb("minus_half", [P, 1])

        def weight_tiles(js, at):
            for j in js:
                for n in range(2):
                    up_hi[n].append(sb(f"w{n}_hi{j}", [P, KT, WIDTH[j]], F32R, at))
                    up_lo[n].append(sb(f"w{n}_lo{j}", [P, KT, WIDTH[j]], F32R, at))
                down_hi.append(sb(f"w2_hi{j}", [P, D], F32R, at))
                down_lo.append(sb(f"w2_lo{j}", [P, D], F32R, at))

        up_hi, up_lo, down_hi, down_lo = [[], []], [[], []], [], []
        weight_tiles(range(EARLY_TILES), ctx)

        with ExitStack() as early:
            const = sb("const", [P, CONST_COLS], at=early)
            wmod_sb = sb("wmod_sb", [P, KT, 6 * D], at=early)
            mask_sb = sb("mask_sb", [P, KT, D], I32, at=early)
            wa = sb("wa", [P, KT, D], at=early)
            wa_hi = sb("wa_hi", [P, KT, D], F32R, at=early)
            wa_lo = sb("wa_lo", [P, KT, D], F32R, at=early)
            lora_raw = sb("lora_raw", [P, LORA_COLS], at=early)
            mask_part = sb("mask_part", [P, KT * NB], at=early)
            block_on = sb("block_on", [P, KT * NB], at=early)
            ct = sb("ct", [P, KT, B], at=early)
            silu_c = sb("silu_c", [P, KT, B], at=early)
            bias_raw = sb("bias_raw", [2, D], at=early)
            bias_parts = sb("bias_parts", [2, D], F32R, at=early)
            ones = sb("ones", [2, P], F32R, at=early)
            ones_f = sb("ones_f", [2, P], at=early)
        weight_tiles(range(EARLY_TILES, HT), ctx)

        acc = [ctx.enter_context(nc.psum_tensor(f"acc{t}", [P, D], F32)) for t in range(T)]
        up_a = ctx.enter_context(nc.psum_tensor("up_a", [P, S], F32))
        up_b = ctx.enter_context(nc.psum_tensor("up_b", [P, S], F32))
        side = [ctx.enter_context(nc.psum_tensor(f"side{n}", [P, 512], F32)) for n in range(2)]
        attn_bank = [*acc, up_a, up_b, acc[0], acc[1]]

        c_loaded = sem("c_loaded")
        const_loaded = sem("const_loaded")
        ident_loaded = sem("ident_loaded")
        bias_loaded = sem("bias_loaded")
        mask_loaded = sem("mask_loaded")
        wa_loaded = sem("wa_loaded")
        lora_loaded = sem("lora_loaded")
        silu_c_ready = sem("silu_c_ready")
        bias_high_ready = sem("bias_high_ready")
        bias_ready = sem("bias_ready")
        ones_set = sem("ones_set")
        ones_ready = sem("ones_ready")
        parts_high_ready = sem("parts_high_ready")
        parts_kept = sem("parts_kept")
        parts_ready = sem("parts_ready")
        mask_summed = sem("mask_summed")
        mask_out = sem("mask_out")
        block_on_ready = sem("block_on_ready")
        wa_masked = sem("wa_masked")
        wa_high_ready = sem("wa_high_ready")
        wa_ready = sem("wa_ready")
        mod_out = sem("mod_out")
        mod_copied = sem("mod_copied")
        mod_ready = sem("mod_ready")
        gate_sign_ready = sem("gate_sign_ready")
        gate_size_ready = sem("gate_size_ready")
        gate_ready = sem("gate_ready")
        gate_spread = sem("gate_spread")
        gate_out = sem("gate_out")
        gate_row_ready = sem("gate_row_ready")
        stats_ready = sem("stats_ready")
        moments_ready = sem("moments_ready")
        exponent_ready = sem("exponent_ready")
        variance_ready = sem("variance_ready")
        rstd_ready = sem("rstd_ready")
        normed = sem("normed")
        turned = sem("turned")
        h_ready = sem("h_ready")
        h_high_ready = sem("h_high_ready")
        h_low_ready = sem("h_low_ready")
        attn_out = sem("attn_out")
        attn_gated = sem("attn_gated")
        x1_ready = sem("x1_ready")
        merge_out = sem("merge_out")
        merged = sem("merged")
        w_high_ready = sem("w_high_ready")
        w_ready = sem("w_ready")
        h1_out = sem("h1_out")
        silu_ready = sem("silu_ready")
        h3_out = sem("h3_out")
        g_ready = sem("g_ready")
        g_high_ready = sem("g_high_ready")
        g_low_ready = sem("g_low_ready")
        down_out = sem("down_out")
        down_gated = sem("down_gated")
        x2_ready = sem("x2_ready")
        stored = sem("stored")
        x_loaded = [sem(f"x_loaded{b}") for b in range(B)]
        wmod_loaded = [sem(f"wmod_loaded{n}") for n in range(len(MOD_PARTS))]
        raw_loaded = [sem(f"raw_loaded{n}") for n in range(SLOTS)]

        side_read = {"mask": block_on_ready, "mod": mod_copied, "gate": gate_row_ready, "norm": h_ready,
                     "merge": merged}

        def f32(ap):
            return ap.bitcast(F32)

        def weight_parts(r):
            j, n = divmod(r, 3)
            if n < 2:
                src = raw[:, r % SLOTS, 0:KT * WIDTH[j]].rearrange("p (k n) -> p k n", k=KT)
                return src, up_hi[n][j][:], up_lo[n][j][:]
            return raw[0:WIDTH[j], r % SLOTS], down_hi[j][0:WIDTH[j]], down_lo[j][0:WIDTH[j]]

        def tile_of(i):
            return (i % TILES) // T, i % T

        block = ctx.enter_context(nc.Block())

        @block.sync
        def _(sp):
            sp.dma_start(xt[:, 0], x_rows[0]).then_inc(x_loaded[0], 16)
            sp.dma_start(mask_sb[:], mask).then_inc(mask_loaded, 16)
            sp.dma_start(wa[:], weight).then_inc(wa_loaded, 16)
            for n, (first, count) in enumerate(MOD_PARTS):
                cols = slice(first * P, (first + count) * P)
                sp.dma_start(wmod_sb[:, :, cols], wmod_rows[:, :, cols]).then_inc(wmod_loaded[n], 16)
                if n == 1:
                    sp.dma_start(xt[:, 1], x_rows[1]).then_inc(x_loaded[1], 16)
            sp.dma_start(lora_raw[:], lora).then_inc(lora_loaded, 16)
            for r in range(3 * HT):
                if r >= SLOTS:
                    sp.wait_ge(w_ready, r - SLOTS + 1)
                sp.dma_start(raw[:, r % SLOTS], ffn[r]).then_inc(raw_loaded[r % SLOTS], 16)
            for n in range(TILES):
                sp.wait_ge(x2_ready, n + 1)
                sp.dma_start(out_rows[n // T, :, n % T], xt[:, n // T, n % T]).then_inc(stored, 16)
            sp.wait_ge(stored, 16 * TILES)

        @block.gpsimd
        def _(pool):
            nc.gpsimd.memset(minus_half[:], -0.5).then_inc(exponent_ready, 1)
            pool.wait_ge(exponent_ready, 1)

            def root(i):
                pool.wait_ge(moments_ready, i + 1)
                nc.gpsimd.tensor_scalar(var_eps[:, i:i + 1], moments[:, i, 1:2], EPS, None,
                                        ALU.add).then_inc(variance_ready, 1)
                pool.wait_ge(variance_ready, i + 1)
                nc.gpsimd.tensor_tensor(rstd[:, i:i + 1], var_eps[:, i:i + 1], minus_half[:],
                                        ALU.pow).then_inc(rstd_ready, 1)

            def low(i):
                b, t = tile_of(i)
                pool.wait_ge(h_high_ready, i + 1)
                nc.gpsimd.tensor_tensor(
                    ht_lo[b][:, :, t * P:(t + 1) * P], work[:, i % WORK].rearrange("p (k s) -> p k s", k=KT),
                    f32(ht_hi[b][:, :, t * P:(t + 1) * P]), ALU.subtract).then_inc(h_low_ready, 1)

            def spread(n):
                kind, b = divmod(n, B)
                pool.wait_ge(gate_ready, kind + 1)
                if kind:
                    pool.wait_ge(attn_gated, T * (b + 1))
                nc.gpsimd.tensor_copy(gate_row[:, b].rearrange("p (k m) -> p k m", k=KT),
                                      gates[:, kind * KT:(kind + 1) * KT, b:b + 1].broadcast_to([P, KT, P])
                                      ).then_inc(gate_spread, 1)

            for i in range(WORK):
                root(i)
            low(0)
            root(3)
            low(1)
            low(2)
            low(3)
            root(4)
            root(5)
            spread(0)
            spread(1)
            low(4)
            root(6)
            low(5)
            root(7)
            low(6)
            low(7)
            root(8)
            root(9)
            low(8)
            root(10)
            low(9)
            for n, (lo, hi) in enumerate(LORA_CUTS):
                keep = KEEP_A if n in (1, 2) else KEEP_B
                pool.wait_ge(parts_high_ready, n + 1)
                nc.gpsimd.tensor_scalar(parts[:, lo:hi], f32(parts[:, lo:hi]), const[:, keep:keep + 1], None,
                                        ALU.mult).then_inc(parts_kept, 1)
                pool.wait_ge(parts_kept, n + 1)
                nc.gpsimd.tensor_tensor(parts[:, lo:hi], f32(parts[:, lo:hi]), lora_raw[:, lo:hi],
                                        ALU.add).then_inc(parts_ready, 1)
            root(11)
            low(10)
            low(11)
            for i in range(TILES + T, NORMS):
                root(i)
                low(i)
            spread(2)
            spread(3)

        @block.scalar
        def _(act):
            act.dma_start(ct[:], c).then_inc(c_loaded, 16)
            act.dma_start(const[:], consts).then_inc(const_loaded, 16)
            act.dma_start(ident[:], identity).then_inc(ident_loaded, 16)
            act.dma_start(bias_raw[:], bias).then_inc(bias_loaded, 16)
            act.wait_ge(c_loaded, 16)
            nc.scalar.activation(silu_c[:], ct[:], ACT.Silu).then_inc(silu_c_ready, 1)
            act.wait_ge(bias_loaded, 16)
            nc.scalar.activation(bias_parts[:], bias_raw[:], ACT.Copy).then_inc(bias_high_ready, 1)
            act.wait_ge(wa_masked, 1)
            nc.scalar.activation(wa_hi[:], wa[:], ACT.Copy).then_inc(wa_high_ready, 1)

            def high(i):
                b, t = tile_of(i)
                act.wait_ge(h_ready, i + 1)
                if i >= TILES:
                    act.wait_ge(attn_out, T * (b + 1))
                nc.scalar.activation(ht_hi[b][:, :, t * P:(t + 1) * P],
                                     work[:, i % WORK].rearrange("p (k s) -> p k s", k=KT),
                                     ACT.Copy).then_inc(h_high_ready, 1)

            def weight_high(r):
                act.wait_ge(merged, r + 1)
                src, dst, _ = weight_parts(r)
                nc.scalar.activation(dst, src, ACT.Copy).then_inc(w_high_ready, 1)

            for i in range(T):
                high(i)
            for i in range(T, TILES + 2):
                high(i)
                if i == TILES - 1:
                    act.wait_ge(lora_loaded, 16)
                    for lo, hi in LORA_CUTS:
                        nc.scalar.activation(parts[:, lo:hi], lora_raw[:, lo:hi], ACT.Copy).then_inc(parts_high_ready, 1)
            weight_high(0)
            high(10)
            weight_high(1)
            weight_high(2)
            high(11)
            for r in range(3, 6):
                weight_high(r)
            for s in range(B * HT):
                w = WIDTH[s % HT]
                more = s + 2 < HT
                if more:
                    weight_high(3 * (s + 2))
                act.wait_ge(h1_out, s + 1)
                if s:
                    act.wait_ge(g_low_ready, s)
                nc.scalar.activation(g[0:w], up_a[0:w], ACT.Silu).then_inc(silu_ready, 1)
                if more:
                    weight_high(3 * (s + 2) + 1)
                act.wait_ge(g_ready, s + 1)
                nc.scalar.activation(g_hi[s % 2][0:w], g[0:w], ACT.Copy).then_inc(g_high_ready, 1)
                if more:
                    weight_high(3 * (s + 2) + 2)
                if s < T:
                    high(TILES + T + s)

        @block.vector
        def _(dve):
            def moment(i):
                b, t = tile_of(i)
                if i < TILES:
                    dve.wait_ge(x_loaded[b], 16)
                else:
                    dve.wait_ge(x1_ready, i - TILES + 1)
                if i >= 2:
                    dve.wait_ge(moments_ready, i - 1)
                nc.vector.bn_stats(stats[:, i % 2], xt[:, b, t]).then_inc(stats_ready, 1)
                dve.wait_ge(stats_ready, i + 1)
                nc.vector.bn_aggr(moments[:, i], stats[:, i % 2]).then_inc(moments_ready, 1)

            def norm(i):
                b, t = tile_of(i)
                dve.wait_ge(rstd_ready, i + 1)
                if i >= WORK:
                    dve.wait_ge(h_low_ready, i - WORK + 1)
                nc.vector.tensor_scalar(work[:, i % WORK], xt[:, b, t], moments[:, i, 0:1], rstd[:, i:i + 1],
                                        ALU.subtract, ALU.mult).then_inc(normed, 1)

            def modulate(i):
                b, t = tile_of(i)
                second = i // TILES
                dve.wait_ge(turned, i + 1)
                src = side[SIDE[("norm", i)] % 2] if i >= T else acc[i]
                for k in range(KT):
                    last = nc.vector.tensor_scalar(
                        work[:, i % WORK, k * P:(k + 1) * P], src[:, k * P:(k + 1) * P],
                        one_plus[:, KT * second + k, b:b + 1],
                        mod[:, (SHIFT_F if second else SHIFT_A) + k, b:b + 1], ALU.mult, ALU.add)
                last.then_inc(h_ready, 1)

            def modulation(n):
                first, count = MOD_PARTS[n]
                dve.wait_ge(mod_out, n + 1)
                nc.vector.tensor_copy(mod[:, first:first + count].rearrange("p n b -> p (n b)"),
                                      side[SIDE[("mod", n)] % 2][:, 0:count * B]).then_inc(mod_copied, 1)
                dve.wait_ge(mod_copied, n + 1)

            def scale_plus_one(first, n):
                nc.vector.tensor_scalar(one_plus[:, n * KT:(n + 1) * KT], mod[:, first:first + KT], 1.0, None,
                                        ALU.add).then_inc(mod_ready, 1)
                dve.wait_ge(mod_ready, n + 1)

            def gate(first, n):
                src = mod[:, first:first + KT]
                nc.vector.tensor_scalar(gate_sign[:], src, 0.0, 2.0, ALU.is_ge, ALU.mult).then_inc(gate_sign_ready, 1)
                nc.vector.scalar_tensor_tensor(gate_size[:], src, -1.0, src, ALU.mult, ALU.max
                                               ).then_inc(gate_size_ready, 1)
                dve.wait_ge(gate_size_ready, 2 * n + 1)
                nc.vector.tensor_scalar(gate_size[:], gate_size[:], GATE_MIN, None, ALU.max
                                        ).then_inc(gate_size_ready, 1)
                dve.wait_ge(gate_sign_ready, n + 1)
                dve.wait_ge(gate_size_ready, 2 * n + 2)
                nc.vector.scalar_tensor_tensor(gates[:, n * KT:(n + 1) * KT], gate_sign[:], -1.0, gate_size[:],
                                               ALU.add, ALU.mult).then_inc(gate_ready, 1)

            def gate_rows(n):
                dve.wait_ge(gate_out, n + 1)
                nc.vector.tensor_copy(gate_row[:, n % B], side[SIDE[("gate", n)] % 2][:]).then_inc(gate_row_ready, 1)
                dve.wait_ge(gate_row_ready, n + 1)

            def attn_end(a):
                b, t = divmod(a, T)
                dve.wait_ge(attn_out, a + 1)
                if a:
                    dve.wait_ge(x1_ready, a)
                nc.vector.tensor_tensor(g[:], attn_bank[a][:], gate_row[:, b], ALU.mult).then_inc(attn_gated, 1)
                dve.wait_ge(attn_gated, a + 1)
                nc.vector.tensor_tensor(xt[:, b, t], g[:], xt[:, b, t], ALU.add).then_inc(x1_ready, 1)

            def merge(r):
                src, _, _ = weight_parts(r)
                rows = WIDTH[r // 3] if r % 3 == 2 else P
                cols = D if r % 3 == 2 else KT * WIDTH[r // 3]
                dve.wait_ge(raw_loaded[r % SLOTS], 16 * (r // SLOTS + 1))
                dve.wait_ge(merge_out, r + 1)
                w = raw[0:rows, r % SLOTS, 0:cols]
                nc.vector.scalar_tensor_tensor(w, side[SIDE[("merge", r)] % 2][0:rows, 0:cols], SCALING, w,
                                               ALU.mult, ALU.add).then_inc(merged, 1)

            def weight_low(r):
                src, high, low = weight_parts(r)
                dve.wait_ge(w_high_ready, r + 1)
                nc.vector.tensor_tensor(low, src, f32(high), ALU.subtract).then_inc(w_ready, 1)

            def down_end(n):
                b, t = divmod(n, T)
                dve.wait_ge(down_out, n + 1)
                if n >= WORK:
                    dve.wait_ge(x2_ready, n - WORK + 1)
                nc.vector.tensor_tensor(work[:, n % WORK], acc[t][:], gate_row[:, b], ALU.mult).then_inc(down_gated, 1)
                dve.wait_ge(down_gated, n + 1)
                nc.vector.tensor_tensor(xt[:, b, t], work[:, n % WORK], xt[:, b, t], ALU.add).then_inc(x2_ready, 1)

            nc.vector.memset(ones_f[:], 1.0).then_inc(ones_set, 1)
            dve.wait_ge(ones_set, 1)
            nc.vector.tensor_copy(ones[:], ones_f[:]).then_inc(ones_ready, 1)
            moment(0)
            moment(1)
            norm(0)
            moment(2)
            norm(1)
            moment(3)
            norm(2)
            dve.wait_ge(const_loaded, 16)
            dve.wait_ge(bias_high_ready, 1)
            nc.vector.scalar_tensor_tensor(bias_parts[:], f32(bias_parts[:]), const[0:2, KEEP_BIAS:KEEP_BIAS + 1],
                                           bias_raw[:], ALU.mult, ALU.add).then_inc(bias_ready, 1)
            dve.wait_ge(mask_loaded, 16)
            nc.vector.tensor_reduce(mask_part[:], mask_sb[:].rearrange("p k (n c) -> p (k n) c", c=BLOCK),
                                    AX.X, ALU.add).then_inc(mask_summed, 1)
            dve.wait_ge(mask_out, 1)
            nc.vector.tensor_scalar(block_on[:], side[SIDE[("mask", 0)] % 2][:, 0:KT * NB], 0.0, None,
                                    ALU.is_gt).then_inc(block_on_ready, 1)
            dve.wait_ge(block_on_ready, 1)
            dve.wait_ge(wa_loaded, 16)
            wa_blocks = wa[:].rearrange("p k (n c) -> p (k n) c", c=BLOCK)
            nc.vector.tensor_tensor(wa_blocks, wa_blocks, block_on[:].unsqueeze(2).broadcast_to([P, KT * NB, BLOCK]),
                                    ALU.mult).then_inc(wa_masked, 1)
            dve.wait_ge(wa_high_ready, 1)
            nc.vector.tensor_tensor(wa_lo[:], wa[:], f32(wa_hi[:]), ALU.subtract).then_inc(wa_ready, 1)
            modulation(0)
            scale_plus_one(SCALE_A, 0)
            modulate(0)
            norm(3)
            modulate(1)
            modulate(2)
            modulate(3)
            moment(4)
            moment(5)
            modulation(1)
            gate(GATE_A, 0)
            norm(4)
            gate_rows(0)
            gate_rows(1)
            attn_end(0)
            modulate(4)
            norm(5)
            moment(6)
            attn_end(1)
            modulate(5)
            norm(6)
            moment(7)
            attn_end(2)
            modulate(6)
            norm(7)
            attn_end(3)
            modulate(7)
            moment(8)
            modulation(2)
            scale_plus_one(SCALE_F, 1)
            gate(GATE_F, 1)
            norm(8)
            moment(9)
            modulate(8)
            norm(9)
            moment(10)
            attn_end(4)
            modulate(9)
            norm(10)
            moment(11)
            merge(0)
            modulate(10)
            norm(11)
            merge(1)
            weight_low(0)
            attn_end(5)
            merge(2)
            weight_low(1)
            modulate(11)
            for r in range(3, 6):
                merge(r)
                weight_low(r - 1)
            attn_end(6)
            attn_end(7)
            moment(12)
            norm(12)
            for s in range(B * HT):
                w = WIDTH[s % HT]
                more = s + 2 < HT
                if s + 2 <= HT:
                    if more:
                        merge(3 * (s + 2))
                    weight_low(3 * (s + 2) - 1)
                if more:
                    merge(3 * (s + 2) + 1)
                    weight_low(3 * (s + 2))
                dve.wait_ge(silu_ready, s + 1)
                dve.wait_ge(h3_out, s + 1)
                nc.vector.tensor_tensor(g[0:w], up_b[0:w], g[0:w], ALU.mult).then_inc(g_ready, 1)
                if more:
                    merge(3 * (s + 2) + 2)
                    weight_low(3 * (s + 2) + 1)
                dve.wait_ge(g_high_ready, s + 1)
                nc.vector.tensor_tensor(g_lo[s % 2][0:w], g[0:w], f32(g_hi[s % 2][0:w]),
                                        ALU.subtract).then_inc(g_low_ready, 1)
                if s < T:
                    modulate(TILES + T + s)
                    if s + 1 < T:
                        moment(TILES + T + s + 1)
                        norm(TILES + T + s + 1)
                elif s < T + B:
                    gate_rows(B + s - T)
                if s == HT:
                    for n in range(T):
                        down_end(n)
            for n in range(T, TILES):
                down_end(n)

        @block.tensor
        def _(pe):
            def free_side(job):
                n = SIDE[job]
                if n >= 2:
                    kind, index = SIDE_JOBS[n - 2]
                    pe.wait_ge(side_read[kind], index + 1)
                return side[n % 2]

            def turn(i):
                dst = free_side(("norm", i)) if i >= T else acc[i]
                pe.wait_ge(normed, i + 1)
                for k in range(KT):
                    last = nc.tensor.transpose(dst[:, k * P:(k + 1) * P], work[:, i % WORK, k * P:(k + 1) * P],
                                               ident[:])
                last.then_inc(turned, 1)

            def modulation(n):
                first, count = MOD_PARTS[n]
                dst = free_side(("mod", n))
                pe.wait_ge(wmod_loaded[n], 16)
                for m in range(count):
                    for k in range(KT):
                        last = nc.tensor.matmul(dst[:, m * B:(m + 1) * B],
                                                wmod_sb[:, k, (first + m) * P:(first + m + 1) * P], silu_c[:, k],
                                                start=(k == 0), stop=(k == KT - 1))
                last.then_inc(mod_out, 1)

            def gate_rows(n):
                dst = free_side(("gate", n))
                pe.wait_ge(gate_spread, n + 1)
                for k in range(KT):
                    last = nc.tensor.transpose(dst[:, k * P:(k + 1) * P], gate_row[:, n % B, k * P:(k + 1) * P],
                                               ident[:])
                last.then_inc(gate_out, 1)

            def attention(a):
                b, t = divmod(a, T)
                dst = attn_bank[a]
                pe.wait_ge(h_low_ready, a + 1)
                if a >= T + 2:
                    pe.wait_ge(attn_gated, a - T - 1)
                nc.tensor.matmul(dst[:], ones[:], bias_parts[:], start=True, stop=False)
                for k in range(KT):
                    hi, lo = (h[b][:, k, t * P:(t + 1) * P] for h in (ht_hi, ht_lo))
                    nc.tensor.matmul(dst[:], hi, wa_hi[:, k], start=False, stop=False)
                    nc.tensor.matmul(dst[:], hi, wa_lo[:, k], start=False, stop=False)
                    last = nc.tensor.matmul(dst[:], lo, wa_hi[:, k], start=False, stop=(k == KT - 1))
                last.then_inc(attn_out, 1)

            def merge(r):
                j, n = divmod(r, 3)
                w = WIDTH[j]
                dst = free_side(("merge", r))
                if n < 2:
                    rows = slice(n * RANKS, (n + 1) * RANKS)
                    for k in range(KT):
                        last = nc.tensor.matmul(dst[:, k * w:(k + 1) * w],
                                                parts[rows, LORA_A13 + k * P:LORA_A13 + (k + 1) * P],
                                                parts[rows, LORA_B13 + j * P:LORA_B13 + j * P + w],
                                                start=True, stop=True)
                else:
                    rows = slice((j % 2) * RANKS, (j % 2 + 1) * RANKS)
                    at = LORA_A2 + (j // 2) * P
                    last = nc.tensor.matmul(dst[0:w], parts[rows, at:at + w], parts[rows, LORA_B2:LORA_B2 + D],
                                            start=True, stop=True)
                last.then_inc(merge_out, 1)

            def up(s, n, dst, signal):
                b, j = divmod(s, HT)
                w = WIDTH[j]
                pe.wait_ge(w_ready, 3 * j + n + 1)
                for k in range(KT):
                    nc.tensor.matmul(dst[0:w], up_hi[n][j][:, k], ht_hi[b][:, k], start=(k == 0), stop=False)
                    nc.tensor.matmul(dst[0:w], up_hi[n][j][:, k], ht_lo[b][:, k], start=False, stop=False)
                    last = nc.tensor.matmul(dst[0:w], up_lo[n][j][:, k], ht_hi[b][:, k], start=False,
                                            stop=(k == KT - 1))
                last.then_inc(signal, 1)

            def down(s, t):
                b, j = divmod(s, HT)
                w = WIDTH[j]
                pe.wait_ge(g_low_ready, s + 1)
                pe.wait_ge(w_ready, 3 * j + 3)
                if j == 0:
                    if b:
                        pe.wait_ge(down_gated, t + 1)
                    else:
                        pe.wait_ge(attn_gated, TILES)
                hi, lo = (h[s % 2][0:w, t * P:(t + 1) * P] for h in (g_hi, g_lo))
                nc.tensor.matmul(acc[t][:], hi, down_hi[j][0:w], start=(j == 0), stop=False)
                nc.tensor.matmul(acc[t][:], hi, down_lo[j][0:w], start=False, stop=False)
                last = nc.tensor.matmul(acc[t][:], lo, down_hi[j][0:w], start=False, stop=(j == HT - 1))
                if j == HT - 1:
                    last.then_inc(down_out, 1)

            pe.wait_ge(ident_loaded, 16)
            for i in range(WORK):
                turn(i)
            pe.wait_ge(const_loaded, 16)
            pe.wait_ge(mask_summed, 1)
            nc.tensor.matmul(free_side(("mask", 0))[:, 0:KT * NB], const[:, BLOCK_ONES:BLOCK_ONES + P], mask_part[:],
                             start=True, stop=True).then_inc(mask_out, 1)
            pe.wait_ge(silu_c_ready, 1)
            modulation(0)
            pe.wait_ge(wa_ready, 1)
            pe.wait_ge(ones_ready, 1)
            pe.wait_ge(bias_ready, 1)
            turn(3)
            attention(0)
            modulation(1)
            attention(1)
            gate_rows(0)
            gate_rows(1)
            attention(2)
            turn(4)
            turn(5)
            attention(3)
            turn(6)
            attention(4)
            turn(7)
            modulation(2)
            attention(5)
            turn(8)
            attention(6)
            turn(9)
            attention(7)
            pe.wait_ge(parts_ready, len(LORA_CUTS))
            merge(0)
            turn(10)
            merge(1)
            merge(2)
            turn(11)
            for r in range(3, 6):
                merge(r)
            pe.wait_ge(h_low_ready, TILES + T)
            pe.wait_ge(attn_gated, T + 2)
            for s in range(B * HT):
                more = s + 2 < HT
                if s == HT:
                    pe.wait_ge(h_low_ready, NORMS)
                if more:
                    merge(3 * (s + 2))
                if s:
                    pe.wait_ge(silu_ready, s)
                up(s, 0, up_a, h1_out)
                if more:
                    merge(3 * (s + 2) + 1)
                if s:
                    pe.wait_ge(g_ready, s)
                up(s, 1, up_b, h3_out)
                if more:
                    merge(3 * (s + 2) + 2)
                if s:
                    for t in range(T):
                        down(s - 1, t)
                if s < T:
                    turn(TILES + T + s)
                elif s < T + B:
                    gate_rows(B + s - T)
            for t in range(T):
                down(B * HT - 1, t)


def launch_inputs(x, mask, weight, bias, w1, w3, w2, a1, b1, a3, b3, a2, b2, c, wmod):
    def by_feature(m):
        return m.reshape(KT, P, -1).transpose(1, 0, 2)

    ffn = np.zeros((3 * HT, P, D), np.float32)
    for j, w in enumerate(WIDTH):
        for n, up in enumerate((w1, w3)):
            ffn[3 * j + n, :, 0:KT * w] = by_feature(up[j * P:j * P + w].T).reshape(P, KT * w)
        ffn[3 * j + 2, 0:w] = w2[:, j * P:j * P + w].T

    def stack(rows):
        return np.tile(rows, (RANKS // R, 1))

    lora = np.zeros((P, LORA_COLS), np.float32)
    for n, (a, b) in enumerate(((a1, b1), (a3, b3))):
        rows = slice(n * RANKS, (n + 1) * RANKS)
        lora[rows, LORA_B13:LORA_B13 + HID] = stack(b.T)
        lora[rows, LORA_A13:LORA_A13 + D] = stack(a)
        lora[rows, LORA_B2:LORA_B2 + D] = stack(b2.T)
    for j, w in enumerate(WIDTH):
        at = LORA_A2 + (j // 2) * P
        lora[(j % 2) * RANKS:(j % 2 + 1) * RANKS, at:at + w] = stack(a2[:, j * P:j * P + w])

    p = np.arange(P)
    consts = np.zeros((P, CONST_COLS), np.float32)
    consts[:, BLOCK_ONES:BLOCK_ONES + P] = p[:, None] // BLOCK == p // BLOCK
    consts[:, KEEP_B] = -(p // (2 * R) % 2)
    consts[:, KEEP_A] = -(p // R % 2)
    consts[:, KEEP_BIAS] = -(p % 2)
    return {
        "x": x.reshape(B * S, D),
        "mask": by_feature(mask.T),
        "weight": by_feature(weight.T),
        "bias": np.tile(bias, (2, 1)),
        "ffn": ffn,
        "lora": lora,
        "c": by_feature(c.T),
        "wmod": wmod,
        "identity": np.eye(P, dtype=np.float32),
        "consts": consts,
    }


def kernel(L0_attn_data, L0_attn_mask, L0_attn_weight, L0_attn_bias, L0_ffn_w1, L0_ffn_w3, L0_ffn_w2,
           L0_ffn_lora_A1, L0_ffn_lora_B1, L0_ffn_lora_A3, L0_ffn_lora_B3, L0_ffn_lora_A2, L0_ffn_lora_B2,
           L0_c, L0_wmod):
    import concourse.bacc as bacc
    from concourse.bass_utils import run_bass_kernel_spmd

    given = (L0_attn_data, L0_attn_mask, L0_attn_weight, L0_attn_bias, L0_ffn_w1, L0_ffn_w3, L0_ffn_w2,
             L0_ffn_lora_A1, L0_ffn_lora_B1, L0_ffn_lora_A3, L0_ffn_lora_B3, L0_ffn_lora_A2, L0_ffn_lora_B2,
             L0_c, L0_wmod)
    nc = bacc.Bacc("TRN2", target_bir_lowering=False, num_devices=1, dynamic_dma_scratch_size=1024)
    arrays, args = {}, {}
    for name, a in launch_inputs(*(np.asarray(g) for g in given)).items():
        a = np.ascontiguousarray(a)
        arrays[f"in_{name}"] = a
        args[name] = nc.dram_tensor(f"in_{name}", a.shape, mybir.dt.from_np(a.dtype), kind="ExternalInput").ap()
    out = nc.dram_tensor("out", (B, S, D), F32, kind="ExternalOutput").ap()
    build(nc, out=out, **args)
    return run_bass_kernel_spmd(nc, [arrays], core_ids=[0]).results[0]["out"]
```

```python
from contextlib import ExitStack

import numpy as np

import concourse.bass as bass
from concourse import mybir

P = 128
ALU = mybir.AluOpType
ACT = mybir.ActivationFunctionType
AX = mybir.AxisListType
F32 = mybir.dt.float32
F32R = mybir.dt.float32r
I32 = mybir.dt.int32

B, S, D, HID, R = 2, 512, 512, 1376, 16
BLOCK = 32
SCALING = 32.0 / 16.0
EPS = 1e-05
GATE_MIN = 0.25
KT = D // P
T = S // P
TILES = B * T
NORMS = 2 * TILES
HT = -(-HID // P)
WIDTH = [min(P, HID - j * P) for j in range(HT)]
NB = D // BLOCK
SLOTS = 5
WORK = 4
EARLY_TILES = 2
RANKS = 4 * R

SHIFT_A, SCALE_A, GATE_A, SHIFT_F, SCALE_F, GATE_F = range(6)
QUAD = 32
BOTH = 0
MOD_PASSES = [[(SHIFT_A, BOTH), (SCALE_A, BOTH)],
              [(GATE_A, 1), (GATE_A, 2), (GATE_F, 1), (GATE_F, 2)],
              [(SHIFT_F, BOTH), (SCALE_F, BOTH)]]

A2_COLS = -(-HT // 2) * P
LORA_B13, LORA_A13, LORA_A2, LORA_B2 = 0, HID, HID + D, HID + D + A2_COLS
LORA_COLS = LORA_B2 + D
LORA_CUTS = [(LORA_B13, LORA_A13), (LORA_A13, LORA_A2), (LORA_A2, LORA_B2), (LORA_B2, LORA_COLS)]

BLOCK_ONES, KEEP_B, KEEP_A, KEEP_BIAS = 0, P, P + 1, P + 2
CONST_COLS = P + 3

MERGES = [("merge", r) for r in range(3 * HT)]


def side_jobs():
    def norm(i):
        return ("norm", i)

    def attn(a):
        return ("attn", a)

    jobs = [("mod", 0), ("cols", 0), ("mask", 0), ("mod", 1), norm(4), norm(5), ("mod", 2), norm(6), ("cols", 1),
            norm(7), attn(4), norm(8), attn(5), norm(9), MERGES[0], norm(10), MERGES[1], norm(11), *MERGES[2:6]]
    for s in range(HT):
        jobs += MERGES[3 * (s + 2):3 * (s + 3)]
        if s < 2:
            jobs.append(attn(T + 2 + s))
        elif s < 2 + T:
            jobs.append(norm(NORMS - T + s - 2))
    return jobs


SIDE_JOBS = side_jobs()
SIDE = {job: n for n, job in enumerate(SIDE_JOBS)}


def build(nc, x, mask, weight, bias, ffn, lora, c, wmod, identity, consts, out):
    x_rows = x.rearrange("(b p t) d -> b p t d", b=B, p=P)
    out_rows = out.rearrange("b (p t) d -> b p t d", p=P)
    wmod_rows = wmod.rearrange("(k p) n -> p k n", p=P)

    with ExitStack() as ctx:
        def sb(name, shape, dt=F32, at=ctx):
            return at.enter_context(nc.sbuf_tensor(name, shape, dt))

        def sem(name):
            return ctx.enter_context(nc.semaphore(name))

        xt = sb("xt", [P, B, T, D])
        ht_hi = [sb(f"ht_hi{b}", [P, KT, S], F32R) for b in range(B)]
        ht_lo = [sb(f"ht_lo{b}", [P, KT, S], F32R) for b in range(B)]
        work = sb("work", [P, WORK, D])
        raw = sb("raw", [P, SLOTS, D])
        g = sb("g", [P, S])
        g_hi = [sb(f"g_hi{n}", [P, S], F32R) for n in range(2)]
        g_lo = [sb(f"g_lo{n}", [P, S], F32R) for n in range(2)]
        gate_row = sb("gate_row", [P, B, D])
        parts = sb("parts", [P, LORA_COLS], F32R)
        shift = sb("shift", [P, 2, KT, B])
        one_plus = sb("one_plus", [P, 2, KT, B])
        stats = sb("stats", [P, 2, 6])
        moments = sb("moments", [P, NORMS, 2])
        var_eps = sb("var_eps", [P, NORMS])
        rstd = sb("rstd", [P, NORMS])
        minus_half = sb("minus_half", [P, 1])

        def weight_tiles(js, at):
            for j in js:
                for n in range(2):
                    up_hi[n].append(sb(f"w{n}_hi{j}", [P, KT, WIDTH[j]], F32R, at))
                    up_lo[n].append(sb(f"w{n}_lo{j}", [P, KT, WIDTH[j]], F32R, at))
                down_hi.append(sb(f"w2_hi{j}", [P, D], F32R, at))
                down_lo.append(sb(f"w2_lo{j}", [P, D], F32R, at))

        up_hi, up_lo, down_hi, down_lo = [[], []], [[], []], [], []
        weight_tiles(range(EARLY_TILES), ctx)

        with ExitStack() as early:
            mask_sb = sb("mask_sb", [P, KT, D], I32, at=early)
            wa = sb("wa", [P, KT, D], at=early)
            wmod_sb = sb("wmod_sb", [P, KT, 6 * D], at=early)
            lora_raw = sb("lora_raw", [P, LORA_COLS], at=early)
            const = sb("const", [P, CONST_COLS], at=early)
            mask_part = sb("mask_part", [P, KT * NB], at=early)
            block_on = sb("block_on", [P, KT * NB], at=early)
            ct = sb("ct", [P, KT, B], at=early)
            silu_c = sb("silu_c", [P, KT, 1 + B, QUAD], at=early)
            mod_rows = sb("mod_rows", [2 * QUAD, D], at=early)
            gated = sb("gated", [P, D], at=early)
            bias_raw = sb("bias_raw", [2, D], at=early)
            wa_hi = [sb(f"wa_hi{k}", [P, D], F32R, at=early) for k in range(KT)]
            wa_lo = [sb(f"wa_lo{k}", [P, D], F32R, at=early) for k in range(KT)]
            gates = sb("gates", [P, D], at=early)
            ident = sb("ident", [P, P], at=early)
            bias_parts = sb("bias_parts", [2, D], F32R, at=early)
            ones = sb("ones", [2, P], F32R, at=early)
        weight_tiles(range(EARLY_TILES, HT), ctx)

        acc = [ctx.enter_context(nc.psum_tensor(f"acc{t}", [P, D], F32)) for t in range(T)]
        up_a = ctx.enter_context(nc.psum_tensor("up_a", [P, S], F32))
        up_b = ctx.enter_context(nc.psum_tensor("up_b", [P, S], F32))
        side = [ctx.enter_context(nc.psum_tensor(f"side{n}", [P, 512], F32)) for n in range(2)]

        c_loaded = sem("c_loaded")
        const_loaded = sem("const_loaded")
        ident_loaded = sem("ident_loaded")
        bias_loaded = sem("bias_loaded")
        mask_loaded = sem("mask_loaded")
        lora_loaded = sem("lora_loaded")
        silu_c_ready = sem("silu_c_ready")
        bias_high_ready = sem("bias_high_ready")
        bias_ready = sem("bias_ready")
        ones_ready = sem("ones_ready")
        parts_high_ready = sem("parts_high_ready")
        parts_kept = sem("parts_kept")
        parts_ready = sem("parts_ready")
        mask_summed = sem("mask_summed")
        mask_out = sem("mask_out")
        block_on_ready = sem("block_on_ready")
        wa_masked = sem("wa_masked")
        wa_high_ready = sem("wa_high_ready")
        wa_ready = sem("wa_ready")
        mod_out = sem("mod_out")
        gates_ready = sem("gates_ready")
        cols_ready = sem("cols_ready")
        cols_out = sem("cols_out")
        gate_rows_read = sem("gate_rows_read")
        mod_rows_ready = sem("mod_rows_ready")
        silu_c_cleared = sem("silu_c_cleared")
        gate_sign_ready = sem("gate_sign_ready")
        gate_row_ready = sem("gate_row_ready")
        stats_ready = sem("stats_ready")
        moments_ready = sem("moments_ready")
        exponent_ready = sem("exponent_ready")
        variance_ready = sem("variance_ready")
        rstd_ready = sem("rstd_ready")
        normed = sem("normed")
        turned = sem("turned")
        h_ready = sem("h_ready")
        h_high_ready = sem("h_high_ready")
        h_low_ready = sem("h_low_ready")
        attn_out = sem("attn_out")
        attn_gated = sem("attn_gated")
        x1_ready = sem("x1_ready")
        merge_out = sem("merge_out")
        merged = sem("merged")
        w_high_ready = sem("w_high_ready")
        w_ready = sem("w_ready")
        h1_out = sem("h1_out")
        silu_ready = sem("silu_ready")
        h3_out = sem("h3_out")
        g_ready = sem("g_ready")
        g_high_ready = sem("g_high_ready")
        g_low_ready = sem("g_low_ready")
        down_out = sem("down_out")
        down_gated = sem("down_gated")
        x2_ready = sem("x2_ready")
        stored = sem("stored")
        x_loaded = [sem(f"x_loaded{b}") for b in range(B)]
        wmod_a_loaded = [sem(f"wmod_a_loaded{k}") for k in range(KT)]
        wmod_loaded = {n: sem(f"wmod_loaded{n}") for n in (GATE_A, GATE_F, SHIFT_F, SCALE_F)}
        wa_loaded = [sem(f"wa_loaded{k}") for k in range(KT)]
        raw_loaded = [sem(f"raw_loaded{n}") for n in range(SLOTS)]

        side_read = {"mask": block_on_ready, "cols": cols_ready, "norm": h_ready, "attn": attn_gated,
                     "merge": merged}

        def f32(ap):
            return ap.bitcast(F32)

        def weight_parts(r):
            j, n = divmod(r, 3)
            if n < 2:
                src = raw[:, r % SLOTS, 0:KT * WIDTH[j]].rearrange("p (k n) -> p k n", k=KT)
                return src, up_hi[n][j][:], up_lo[n][j][:]
            return raw[0:WIDTH[j], r % SLOTS], down_hi[j][0:WIDTH[j]], down_lo[j][0:WIDTH[j]]

        def tile_of(i):
            return (i % TILES) // T, i % T

        block = ctx.enter_context(nc.Block())

        @block.sync
        def _(sp):
            sp.dma_start(xt[:, 0], x_rows[0]).then_inc(x_loaded[0], 16)
            for k in range(KT):
                sp.dma_start(wmod_sb[:, k, 0:2 * D], wmod_rows[:, k, 0:2 * D]).then_inc(wmod_a_loaded[k], 16)
            sp.dma_start(mask_sb[:], mask).then_inc(mask_loaded, 16)
            for k in range(KT):
                sp.dma_start(wa[:, k], weight[:, k]).then_inc(wa_loaded[k], 16)

            def load_vector(n):
                cols = slice(n * D, (n + 1) * D)
                sp.dma_start(wmod_sb[:, :, cols], wmod_rows[:, :, cols]).then_inc(wmod_loaded[n], 16)

            load_vector(GATE_A)
            load_vector(GATE_F)
            sp.dma_start(xt[:, 1], x_rows[1]).then_inc(x_loaded[1], 16)
            load_vector(SHIFT_F)
            load_vector(SCALE_F)
            sp.dma_start(lora_raw[:], lora).then_inc(lora_loaded, 16)
            for r in range(3 * HT):
                if r >= SLOTS:
                    sp.wait_ge(w_ready, r - SLOTS + 1)
                sp.dma_start(raw[:, r % SLOTS], ffn[r]).then_inc(raw_loaded[r % SLOTS], 16)
            for n in range(TILES):
                sp.wait_ge(x2_ready, n + 1)
                sp.dma_start(out_rows[n // T, :, n % T], xt[:, n // T, n % T]).then_inc(stored, 16)
            sp.wait_ge(stored, 16 * TILES)

        @block.gpsimd
        def _(pool):
            nc.gpsimd.memset(silu_c[:], 0.0).then_inc(silu_c_cleared, 1)
            nc.gpsimd.memset(minus_half[:], -0.5).then_inc(exponent_ready, 1)
            pool.wait_ge(exponent_ready, 1)

            def root(i):
                pool.wait_ge(moments_ready, i + 1)
                nc.gpsimd.tensor_scalar(var_eps[:, i:i + 1], moments[:, i, 1:2], EPS, None,
                                        ALU.add).then_inc(variance_ready, 1)
                pool.wait_ge(variance_ready, i + 1)
                nc.gpsimd.tensor_tensor(rstd[:, i:i + 1], var_eps[:, i:i + 1], minus_half[:],
                                        ALU.pow).then_inc(rstd_ready, 1)

            def low(i):
                b, t = tile_of(i)
                pool.wait_ge(h_high_ready, i + 1)
                nc.gpsimd.tensor_tensor(
                    ht_lo[b][:, :, t * P:(t + 1) * P], work[:, i % WORK].rearrange("p (k s) -> p k s", k=KT),
                    f32(ht_hi[b][:, :, t * P:(t + 1) * P]), ALU.subtract).then_inc(h_low_ready, 1)

            def gate_rows(n):
                pool.wait_ge(gates_ready, 1)
                pool.wait_ge(h_low_ready, T if n < B else TILES + T)
                if n >= B:
                    pool.wait_ge(attn_gated, T * (n - B + 1))
                nc.gpsimd.partition_broadcast(gate_row[:, n % B], gates[n * QUAD:n * QUAD + 1]
                                              ).then_inc(gate_row_ready, 1)
                pool.wait_ge(gate_row_ready, n + 1)

            for i in range(T):
                root(i)
            for i in range(T):
                low(i)
            gate_rows(0)
            gate_rows(1)
            root(4)
            root(5)
            root(6)
            low(4)
            root(7)
            root(8)
            low(5)
            root(9)
            low(6)
            root(10)
            root(11)
            for i in range(7, 12):
                low(i)
            for i in range(TILES + T, NORMS):
                root(i)
            pool.wait_ge(rstd_ready, NORMS)
            gate_rows(2)
            gate_rows(3)
            for i in range(TILES + T, NORMS):
                low(i)

        @block.scalar
        def _(act):
            act.dma_start(ct[:], c).then_inc(c_loaded, 16)
            act.dma_start(ident[:], identity).then_inc(ident_loaded, 16)
            act.dma_start(const[:], consts).then_inc(const_loaded, 16)
            act.dma_start(bias_raw[:], bias).then_inc(bias_loaded, 16)
            act.wait_ge(c_loaded, 16)
            act.wait_ge(silu_c_cleared, 1)
            nc.scalar.activation(silu_c[:, :, BOTH, 0:B], ct[:], ACT.Silu).then_inc(silu_c_ready, 1)
            nc.scalar.activation(silu_c[:, :, 1:1 + B, 0], ct[:], ACT.Silu).then_inc(silu_c_ready, 1)
            act.wait_ge(bias_loaded, 16)
            nc.scalar.activation(bias_parts[:], bias_raw[:], ACT.Copy).then_inc(bias_high_ready, 1)

            def modulation(n):
                act.wait_ge(mod_out, 2 * n + 1)
                if n:
                    act.wait_ge(cols_out, n)
                nc.scalar.activation(mod_rows[:], side[SIDE[("mod", 2 * n)] % 2][0:2 * QUAD], ACT.Copy
                                     ).then_inc(mod_rows_ready, 1)

            def modulate(i):
                b, t = tile_of(i)
                second = i // TILES
                act.wait_ge(turned, i + 1)
                act.wait_ge(cols_ready, second + 1)
                src = side[SIDE[("norm", i)] % 2] if i >= T else acc[i]
                for k in range(KT):
                    last = nc.scalar.activation(
                        work[:, i % WORK, k * P:(k + 1) * P], src[:, k * P:(k + 1) * P], ACT.Identity,
                        bias=shift[:, second, k, b:b + 1], scale=one_plus[:, second, k, b:b + 1])
                last.then_inc(h_ready, 1)

            def high(i):
                b, t = tile_of(i)
                act.wait_ge(h_ready, i + 1)
                if i >= TILES:
                    act.wait_ge(attn_out, T * (b + 1))
                nc.scalar.activation(ht_hi[b][:, :, t * P:(t + 1) * P],
                                     work[:, i % WORK].rearrange("p (k s) -> p k s", k=KT),
                                     ACT.Copy).then_inc(h_high_ready, 1)

            def weight_high(r):
                act.wait_ge(merged, r + 1)
                src, dst, _ = weight_parts(r)
                nc.scalar.activation(dst, src, ACT.Copy).then_inc(w_high_ready, 1)

            modulation(0)
            for i in range(2):
                modulate(i)
                high(i)
            for k in range(KT):
                act.wait_ge(wa_masked, k + 1)
                nc.scalar.activation(wa_hi[k][:], wa[:, k], ACT.Copy).then_inc(wa_high_ready, 1)
            for i in range(2, T):
                modulate(i)
                high(i)
            act.wait_ge(mod_out, 2)
            src = side[SIDE[("mod", 1)] % 2]
            nc.scalar.activation(gated[:], src[:], ACT.Copy).then_inc(gate_rows_read, 1)
            nc.scalar.activation(g[:], src[:], ACT.Abs, scale=2.0).then_inc(gate_rows_read, 1)
            modulate(4)
            high(4)
            modulate(5)
            high(5)
            modulation(1)
            modulate(6)
            high(6)
            modulate(7)
            high(7)
            act.wait_ge(lora_loaded, 16)
            for lo, hi in LORA_CUTS:
                nc.scalar.activation(parts[:, lo:hi], lora_raw[:, lo:hi], ACT.Copy).then_inc(parts_high_ready, 1)
            for i in (8, 9):
                modulate(i)
                high(i)
            weight_high(0)
            modulate(10)
            high(10)
            weight_high(1)
            modulate(11)
            high(11)
            for r in range(2, 6):
                weight_high(r)
            for s in range(B * HT):
                w = WIDTH[s % HT]
                more = s + 2 < HT
                if more:
                    weight_high(3 * (s + 2))
                act.wait_ge(h1_out, s + 1)
                if s:
                    act.wait_ge(g_low_ready, s)
                nc.scalar.activation(g[0:w], up_a[0:w], ACT.Silu).then_inc(silu_ready, 1)
                if more:
                    weight_high(3 * (s + 2) + 1)
                act.wait_ge(g_ready, s + 1)
                nc.scalar.activation(g_hi[s % 2][0:w], g[0:w], ACT.Copy).then_inc(g_high_ready, 1)
                if more:
                    weight_high(3 * (s + 2) + 2)
                if 2 <= s < 2 + T:
                    modulate(TILES + T + s - 2)
                    high(TILES + T + s - 2)

        @block.vector
        def _(dve):
            def moment(i):
                b, t = tile_of(i)
                if i < TILES:
                    dve.wait_ge(x_loaded[b], 16)
                else:
                    dve.wait_ge(x1_ready, i - TILES + 1)
                if i >= 2:
                    dve.wait_ge(moments_ready, i - 1)
                nc.vector.bn_stats(stats[:, i % 2], xt[:, b, t]).then_inc(stats_ready, 1)
                dve.wait_ge(stats_ready, i + 1)
                nc.vector.bn_aggr(moments[:, i], stats[:, i % 2]).then_inc(moments_ready, 1)

            def norm(i):
                b, t = tile_of(i)
                dve.wait_ge(rstd_ready, i + 1)
                if i >= WORK:
                    dve.wait_ge(h_low_ready, i - WORK + 1)
                nc.vector.tensor_scalar(work[:, i % WORK], xt[:, b, t], moments[:, i, 0:1], rstd[:, i:i + 1],
                                        ALU.subtract, ALU.mult).then_inc(normed, 1)

            def columns(n):
                dve.wait_ge(cols_out, n + 1)
                src = side[SIDE[("cols", n)] % 2][:, 0:KT * 2 * QUAD].rearrange("p (k g b) -> p k g b", k=KT, g=2)
                nc.vector.tensor_copy(shift[:, n], src[:, :, 0, 0:B])
                nc.vector.tensor_scalar(one_plus[:, n], src[:, :, 1, 0:B], 1.0, None, ALU.add
                                        ).then_inc(cols_ready, 1)

            def attn_end(a):
                b, t = divmod(a, T)
                dve.wait_ge(attn_out, a + 1)
                if a:
                    dve.wait_ge(x1_ready, a)
                dve.wait_ge(gate_row_ready, b + 1)
                src = side[SIDE[("attn", a)] % 2] if a >= T else acc[a]
                nc.vector.tensor_tensor(gated[:], src[:], gate_row[:, b], ALU.mult).then_inc(attn_gated, 1)
                dve.wait_ge(attn_gated, a + 1)
                nc.vector.tensor_tensor(xt[:, b, t], gated[:], xt[:, b, t], ALU.add).then_inc(x1_ready, 1)

            def merge(r):
                src, _, _ = weight_parts(r)
                rows = WIDTH[r // 3] if r % 3 == 2 else P
                cols = D if r % 3 == 2 else KT * WIDTH[r // 3]
                dve.wait_ge(raw_loaded[r % SLOTS], 16 * (r // SLOTS + 1))
                dve.wait_ge(merge_out, r + 1)
                w = raw[0:rows, r % SLOTS, 0:cols]
                nc.vector.scalar_tensor_tensor(w, side[SIDE[("merge", r)] % 2][0:rows, 0:cols], SCALING, w,
                                               ALU.mult, ALU.add).then_inc(merged, 1)

            def weight_low(r):
                src, high, low = weight_parts(r)
                dve.wait_ge(w_high_ready, r + 1)
                nc.vector.tensor_tensor(low, src, f32(high), ALU.subtract).then_inc(w_ready, 1)

            def down_end(n):
                b, t = divmod(n, T)
                dve.wait_ge(down_out, n + 1)
                dve.wait_ge(gate_row_ready, B + b + 1)
                if n >= WORK:
                    dve.wait_ge(x2_ready, n - WORK + 1)
                nc.vector.tensor_tensor(work[:, n % WORK], acc[t][:], gate_row[:, b], ALU.mult).then_inc(down_gated, 1)
                dve.wait_ge(down_gated, n + 1)
                nc.vector.tensor_tensor(xt[:, b, t], work[:, n % WORK], xt[:, b, t], ALU.add).then_inc(x2_ready, 1)

            moment(0)
            moment(1)
            norm(0)
            moment(2)
            norm(1)
            moment(3)
            norm(2)
            norm(3)
            dve.wait_ge(const_loaded, 16)
            nc.vector.tensor_scalar(ones[:], const[0:2, 0:P], 0.0, 1.0, ALU.mult, ALU.add).then_inc(ones_ready, 1)
            dve.wait_ge(bias_high_ready, 1)
            nc.vector.scalar_tensor_tensor(bias_parts[:], f32(bias_parts[:]), const[0:2, KEEP_BIAS:KEEP_BIAS + 1],
                                           bias_raw[:], ALU.mult, ALU.add).then_inc(bias_ready, 1)
            columns(0)
            dve.wait_ge(mask_loaded, 16)
            nc.vector.tensor_reduce(mask_part[:], mask_sb[:].rearrange("p k (n c) -> p (k n) c", c=BLOCK),
                                    AX.X, ALU.add).then_inc(mask_summed, 1)
            dve.wait_ge(mask_out, 1)
            nc.vector.tensor_scalar(block_on[:], side[SIDE[("mask", 0)] % 2][:, 0:KT * NB], 0.0, None,
                                    ALU.is_gt).then_inc(block_on_ready, 1)
            dve.wait_ge(block_on_ready, 1)

            def mask_weight(k):
                dve.wait_ge(wa_loaded[k], 16)
                blocks = wa[:, k].rearrange("p (n c) -> p n c", c=BLOCK)
                nc.vector.tensor_tensor(blocks, blocks,
                                        block_on[:, k * NB:(k + 1) * NB].unsqueeze(2).broadcast_to([P, NB, BLOCK]),
                                        ALU.mult).then_inc(wa_masked, 1)

            mask_weight(0)
            for k in range(KT):
                if k + 1 < KT:
                    mask_weight(k + 1)
                dve.wait_ge(wa_high_ready, k + 1)
                nc.vector.tensor_tensor(wa_lo[k][:], wa[:, k], f32(wa_hi[k][:]), ALU.subtract).then_inc(wa_ready, 1)
            dve.wait_ge(gate_rows_read, 2)
            nc.vector.tensor_scalar(gated[:], gated[:], 0.0, -0.5, ALU.is_ge, ALU.add
                                    ).then_inc(gate_sign_ready, 1)
            dve.wait_ge(gate_sign_ready, 1)
            nc.vector.scalar_tensor_tensor(gates[:], g[:], 2 * GATE_MIN, gated[:], ALU.max, ALU.mult
                                           ).then_inc(gates_ready, 1)
            dve.wait_ge(gates_ready, 1)
            moment(4)
            norm(4)
            moment(5)
            norm(5)
            attn_end(0)
            moment(6)
            norm(6)
            attn_end(1)
            moment(7)
            norm(7)
            moment(8)
            attn_end(2)
            moment(9)
            attn_end(3)
            moment(10)
            moment(11)
            columns(1)
            norm(8)
            norm(9)
            for n, (lo, hi) in enumerate(LORA_CUTS):
                keep = KEEP_A if n in (1, 2) else KEEP_B
                dve.wait_ge(parts_high_ready, n + 1)
                nc.vector.scalar_tensor_tensor(parts[:, lo:hi], f32(parts[:, lo:hi]), const[:, keep:keep + 1],
                                               lora_raw[:, lo:hi], ALU.mult, ALU.add).then_inc(parts_ready, 1)
            attn_end(4)
            norm(10)
            attn_end(5)
            norm(11)
            merge(0)
            for r in range(1, 6):
                merge(r)
                weight_low(r - 1)
            moment(12)
            norm(12)
            moment(13)
            norm(13)
            for s in range(B * HT):
                w = WIDTH[s % HT]
                more = s + 2 < HT
                if s == T + 2:
                    dve.wait_ge(gate_row_ready, 2 * B)
                if s + 2 <= HT:
                    if more:
                        merge(3 * (s + 2))
                    weight_low(3 * (s + 2) - 1)
                if more:
                    merge(3 * (s + 2) + 1)
                    weight_low(3 * (s + 2))
                dve.wait_ge(silu_ready, s + 1)
                dve.wait_ge(h3_out, s + 1)
                nc.vector.tensor_tensor(g[0:w], up_b[0:w], g[0:w], ALU.mult).then_inc(g_ready, 1)
                if more:
                    merge(3 * (s + 2) + 2)
                    weight_low(3 * (s + 2) + 1)
                dve.wait_ge(g_high_ready, s + 1)
                nc.vector.tensor_tensor(g_lo[s % 2][0:w], g[0:w], f32(g_hi[s % 2][0:w]),
                                        ALU.subtract).then_inc(g_low_ready, 1)
                if s < 2:
                    attn_end(T + 2 + s)
                    moment(TILES + T + 2 + s)
                    norm(TILES + T + 2 + s)
                if s == HT:
                    for n in range(T):
                        down_end(n)
            for n in range(T, TILES):
                down_end(n)

        @block.tensor
        def _(pe):
            def free_side(job):
                n = SIDE[job]
                if n >= 2:
                    kind, index = SIDE_JOBS[n - 2]
                    if kind == "mod":
                        pe.wait_ge(*((gate_rows_read, 2) if index == 1 else (mod_rows_ready, index // 2 + 1)))
                    else:
                        pe.wait_ge(side_read[kind], index + 1)
                return side[n % 2]

            def turn(i):
                dst = free_side(("norm", i)) if i >= T else acc[i]
                pe.wait_ge(normed, i + 1)
                for k in range(KT):
                    last = nc.tensor.transpose(dst[:, k * P:(k + 1) * P], work[:, i % WORK, k * P:(k + 1) * P],
                                               ident[:])
                last.then_inc(turned, 1)

            def modulation(n):
                dst = free_side(("mod", n))
                for k in range(KT):
                    if n == 0:
                        pe.wait_ge(wmod_a_loaded[k], 16)
                    for q, (vector, variant) in enumerate(MOD_PASSES[n]):
                        if n and k == 0:
                            pe.wait_ge(wmod_loaded[vector], 16)
                        last = nc.tensor.matmul(dst[q * QUAD:(q + 1) * QUAD], silu_c[:, k, variant],
                                                wmod_sb[:, k, vector * D:(vector + 1) * D],
                                                start=(k == 0), stop=(k == KT - 1))
                last.then_inc(mod_out, 1)

            def columns(n):
                dst = free_side(("cols", n))
                pe.wait_ge(mod_rows_ready, n + 1)
                for k in range(KT):
                    last = nc.tensor.transpose(dst[:, k * 2 * QUAD:(k + 1) * 2 * QUAD],
                                               mod_rows[:, k * P:(k + 1) * P], ident[0:2 * QUAD, 0:2 * QUAD])
                last.then_inc(cols_out, 1)

            def attention(a):
                b, t = divmod(a, T)
                dst = free_side(("attn", a)) if a >= T else acc[a]
                pe.wait_ge(h_low_ready, a + 1)
                nc.tensor.matmul(dst[:], ones[:], bias_parts[:], start=True, stop=False)
                for k in range(KT):
                    if a == 0:
                        pe.wait_ge(wa_ready, k + 1)
                    hi, lo = (h[b][:, k, t * P:(t + 1) * P] for h in (ht_hi, ht_lo))
                    nc.tensor.matmul(dst[:], hi, wa_hi[k][:], start=False, stop=False)
                    nc.tensor.matmul(dst[:], hi, wa_lo[k][:], start=False, stop=False)
                    last = nc.tensor.matmul(dst[:], lo, wa_hi[k][:], start=False, stop=(k == KT - 1))
                last.then_inc(attn_out, 1)

            def merge(r):
                j, n = divmod(r, 3)
                w = WIDTH[j]
                dst = free_side(("merge", r))
                if n < 2:
                    rows = slice(n * RANKS, (n + 1) * RANKS)
                    for k in range(KT):
                        last = nc.tensor.matmul(dst[:, k * w:(k + 1) * w],
                                                parts[rows, LORA_A13 + k * P:LORA_A13 + (k + 1) * P],
                                                parts[rows, LORA_B13 + j * P:LORA_B13 + j * P + w],
                                                start=True, stop=True)
                else:
                    rows = slice((j % 2) * RANKS, (j % 2 + 1) * RANKS)
                    at = LORA_A2 + (j // 2) * P
                    last = nc.tensor.matmul(dst[0:w], parts[rows, at:at + w], parts[rows, LORA_B2:LORA_B2 + D],
                                            start=True, stop=True)
                last.then_inc(merge_out, 1)

            def up(s, n, dst, signal):
                b, j = divmod(s, HT)
                w = WIDTH[j]
                pe.wait_ge(w_ready, 3 * j + n + 1)
                for k in range(KT):
                    nc.tensor.matmul(dst[0:w], up_hi[n][j][:, k], ht_hi[b][:, k], start=(k == 0), stop=False)
                    nc.tensor.matmul(dst[0:w], up_hi[n][j][:, k], ht_lo[b][:, k], start=False, stop=False)
                    last = nc.tensor.matmul(dst[0:w], up_lo[n][j][:, k], ht_hi[b][:, k], start=False,
                                            stop=(k == KT - 1))
                last.then_inc(signal, 1)

            def down(s, t):
                b, j = divmod(s, HT)
                w = WIDTH[j]
                pe.wait_ge(g_low_ready, s + 1)
                pe.wait_ge(w_ready, 3 * j + 3)
                if j == 0:
                    pe.wait_ge(*((down_gated, t + 1) if b else (attn_gated, t + 1)))
                hi, lo = (h[s % 2][0:w, t * P:(t + 1) * P] for h in (g_hi, g_lo))
                nc.tensor.matmul(acc[t][:], hi, down_hi[j][0:w], start=(j == 0), stop=False)
                nc.tensor.matmul(acc[t][:], hi, down_lo[j][0:w], start=False, stop=False)
                last = nc.tensor.matmul(acc[t][:], lo, down_hi[j][0:w], start=False, stop=(j == HT - 1))
                if j == HT - 1:
                    last.then_inc(down_out, 1)

            pe.wait_ge(ident_loaded, 16)
            for i in range(T):
                turn(i)
            pe.wait_ge(silu_c_ready, 2)
            modulation(0)
            columns(0)
            pe.wait_ge(const_loaded, 16)
            pe.wait_ge(mask_summed, 1)
            nc.tensor.matmul(free_side(("mask", 0))[:, 0:KT * NB], const[:, BLOCK_ONES:BLOCK_ONES + P], mask_part[:],
                             start=True, stop=True).then_inc(mask_out, 1)
            pe.wait_ge(ones_ready, 1)
            pe.wait_ge(bias_ready, 1)
            attention(0)
            attention(1)
            modulation(1)
            attention(2)
            turn(4)
            attention(3)
            turn(5)
            modulation(2)
            turn(6)
            columns(1)
            turn(7)
            attention(4)
            turn(8)
            attention(5)
            turn(9)
            pe.wait_ge(parts_ready, len(LORA_CUTS))
            merge(0)
            turn(10)
            merge(1)
            turn(11)
            for r in range(2, 6):
                merge(r)
            pe.wait_ge(h_low_ready, TILES + T)
            for s in range(B * HT):
                more = s + 2 < HT
                if s == HT:
                    pe.wait_ge(h_low_ready, NORMS)
                if more:
                    merge(3 * (s + 2))
                if s:
                    pe.wait_ge(silu_ready, s)
                up(s, 0, up_a, h1_out)
                if more:
                    merge(3 * (s + 2) + 1)
                if s:
                    pe.wait_ge(g_ready, s)
                up(s, 1, up_b, h3_out)
                if more:
                    merge(3 * (s + 2) + 2)
                if s:
                    for t in range(T):
                        down(s - 1, t)
                if s < 2:
                    attention(T + 2 + s)
                elif s < 2 + T:
                    turn(TILES + T + s - 2)
            for t in range(T):
                down(B * HT - 1, t)


def launch_inputs(x, mask, weight, bias, w1, w3, w2, a1, b1, a3, b3, a2, b2, c, wmod):
    def by_feature(m):
        return m.reshape(KT, P, -1).transpose(1, 0, 2)

    ffn = np.zeros((3 * HT, P, D), np.float32)
    for j, w in enumerate(WIDTH):
        for n, up in enumerate((w1, w3)):
            ffn[3 * j + n, :, 0:KT * w] = by_feature(up[j * P:j * P + w].T).reshape(P, KT * w)
        ffn[3 * j + 2, 0:w] = w2[:, j * P:j * P + w].T

    def stack(rows):
        return np.tile(rows, (RANKS // R, 1))

    lora = np.zeros((P, LORA_COLS), np.float32)
    for n, (a, b) in enumerate(((a1, b1), (a3, b3))):
        rows = slice(n * RANKS, (n + 1) * RANKS)
        lora[rows, LORA_B13:LORA_B13 + HID] = stack(b.T)
        lora[rows, LORA_A13:LORA_A13 + D] = stack(a)
        lora[rows, LORA_B2:LORA_B2 + D] = stack(b2.T)
    for j, w in enumerate(WIDTH):
        at = LORA_A2 + (j // 2) * P
        lora[(j % 2) * RANKS:(j % 2 + 1) * RANKS, at:at + w] = stack(a2[:, j * P:j * P + w])

    p = np.arange(P)
    consts = np.zeros((P, CONST_COLS), np.float32)
    consts[:, BLOCK_ONES:BLOCK_ONES + P] = p[:, None] // BLOCK == p // BLOCK
    consts[:, KEEP_B] = -(p // (2 * R) % 2)
    consts[:, KEEP_A] = -(p // R % 2)
    consts[:, KEEP_BIAS] = -(p % 2)
    return {
        "x": x.reshape(B * S, D),
        "mask": by_feature(mask.T),
        "weight": by_feature(weight.T),
        "bias": np.tile(bias, (2, 1)),
        "ffn": ffn,
        "lora": lora,
        "c": by_feature(c.T),
        "wmod": wmod,
        "identity": np.eye(P, dtype=np.float32),
        "consts": consts,
    }


def kernel(L0_attn_data, L0_attn_mask, L0_attn_weight, L0_attn_bias, L0_ffn_w1, L0_ffn_w3, L0_ffn_w2,
           L0_ffn_lora_A1, L0_ffn_lora_B1, L0_ffn_lora_A3, L0_ffn_lora_B3, L0_ffn_lora_A2, L0_ffn_lora_B2,
           L0_c, L0_wmod):
    import concourse.bacc as bacc
    from concourse.bass_utils import run_bass_kernel_spmd

    given = (L0_attn_data, L0_attn_mask, L0_attn_weight, L0_attn_bias, L0_ffn_w1, L0_ffn_w3, L0_ffn_w2,
             L0_ffn_lora_A1, L0_ffn_lora_B1, L0_ffn_lora_A3, L0_ffn_lora_B3, L0_ffn_lora_A2, L0_ffn_lora_B2,
             L0_c, L0_wmod)
    nc = bacc.Bacc("TRN2", target_bir_lowering=False, num_devices=1, dynamic_dma_scratch_size=1024)
    arrays, args = {}, {}
    for name, a in launch_inputs(*(np.asarray(g) for g in given)).items():
        a = np.ascontiguousarray(a)
        arrays[f"in_{name}"] = a
        args[name] = nc.dram_tensor(f"in_{name}", a.shape, mybir.dt.from_np(a.dtype), kind="ExternalInput").ap()
    out = nc.dram_tensor("out", (B, S, D), F32, kind="ExternalOutput").ap()
    build(nc, out=out, **args)
    return run_bass_kernel_spmd(nc, [arrays], core_ids=[0]).results[0]["out"]
```

```python
from contextlib import ExitStack

import numpy as np

import concourse.bass as bass
from concourse import mybir

P = 128
ALU = mybir.AluOpType
ACT = mybir.ActivationFunctionType
AX = mybir.AxisListType
F32 = mybir.dt.float32
F32R = mybir.dt.float32r
I32 = mybir.dt.int32

B, S, D, HID, R = 2, 512, 512, 1376, 16
BLOCK = 32
SCALING = 32.0 / 16.0
EPS = 1e-05
GATE_MIN = 0.25
KT = D // P
T = S // P
TILES = B * T
NORMS = 2 * TILES
HT = -(-HID // P)
WIDTH = [min(P, HID - j * P) for j in range(HT)]
NB = D // BLOCK
SLOTS = 4
WORK = 4
EARLY_TILES = 2
WARM_MATMULS = 16
RANKS = 4 * R

SHIFT_A, SCALE_A, GATE_A, SHIFT_F, SCALE_F, GATE_F = range(6)
QUAD = 32
BOTH = 0
MOD_PASSES = [[(SHIFT_A, BOTH), (SCALE_A, BOTH)],
              [(GATE_A, 1), (GATE_A, 2)],
              [(SHIFT_F, BOTH), (SCALE_F, BOTH), (GATE_F, 1), (GATE_F, 2)]]

A2_COLS = -(-HT // 2) * P
LORA_B2, LORA_B13, LORA_A13, LORA_A2 = 0, D, D + HID, D + HID + D
LORA_COLS = LORA_A2 + A2_COLS
LORA_EARLY = 2
LORA_CUTS = [(LORA_B2, LORA_B13 + 2 * P), (LORA_A13, LORA_A2 + P),
             (LORA_B13 + 2 * P, LORA_A13), (LORA_A2 + P, LORA_COLS)]

BLOCK_ONES, KEEP_B, KEEP_A, KEEP_BIAS = 0, P, P + 1, P + 2
HALF_ON = P + 3
CONST_COLS = P + 5

MERGES = [("merge", r) for r in range(3 * HT)]

STEP_TURNS = {2: (8,), 3: (9,), 4: (10,), 5: (11,), 7: (12, 13), 8: (14, 15)}
STEP_ATTN = {3: 4, 4: 5, 5: 6, 6: 7}
STEP_MOMENTS = {1: (8, 9), 2: (10,), 3: (11, 12), 4: (13,), 5: (14,), 6: (15,)}
STEP_GATES_READ = 7
MAKER = {"h": {5: "dve", 7: "dve"}, "high": {5: "dve", 6: "dve"}, "low": {n: "dve" for n in (1, 2, 3, 6, 7)}}
POOL_ADDS = {"x1": (0, 1, 2), "x2": (T, T + 2)}


def side_jobs():
    jobs = [("mod", 0), ("mask", 0), ("cols", 0), ("mod", 1), *MERGES[0:2], ("cols", 1), MERGES[2]]
    for s in range(HT):
        jobs += MERGES[3 * (s + 1):3 * (s + 2)]
        jobs += [("norm", n) for n in STEP_TURNS.get(s, ())]
        if s in STEP_ATTN:
            jobs.append(("attn", STEP_ATTN[s]))
    return jobs


SIDE_JOBS = side_jobs()
SIDE = {job: n for n, job in enumerate(SIDE_JOBS)}


def build(nc, x, mask, weight, bias, ffn, lora, c, wmod, identity, consts, out):
    x_rows = x.rearrange("(b p t) d -> b p t d", b=B, p=P)
    out_rows = out.rearrange("b (p t) d -> b p t d", p=P)
    wmod_rows = wmod.rearrange("(k p) n -> p k n", p=P)

    with ExitStack() as ctx:
        def sb(name, shape, dt=F32, at=ctx):
            return at.enter_context(nc.sbuf_tensor(name, shape, dt))

        def sem(name):
            return ctx.enter_context(nc.semaphore(name))

        xt = sb("xt", [P, B, T, D])
        ht_hi = [sb(f"ht_hi{b}", [P, KT, S], F32R) for b in range(B)]
        ht_lo = [sb(f"ht_lo{b}", [P, KT, S], F32R) for b in range(B)]
        work = sb("work", [P, WORK, D])
        raw = sb("raw", [P, SLOTS, D])
        g = sb("g", [P, S])
        g_hi = [sb(f"g_hi{n}", [P, S], F32R) for n in range(2)]
        g_lo = [sb(f"g_lo{n}", [P, S], F32R) for n in range(2)]
        gate_row = sb("gate_row", [P, B, D])
        parts = sb("parts", [P, LORA_COLS], F32R)
        b13 = [sb(f"b13_{n}", [P, 2, P], F32R) for n in range(2)]
        shift = sb("shift", [P, 2, KT, B])
        one_plus = sb("one_plus", [P, 2, KT, B])
        stats = sb("stats", [P, 2, 6])
        moments = sb("moments", [P, NORMS, 2])
        var_eps = sb("var_eps", [P, NORMS])
        rstd = sb("rstd", [P, NORMS])
        factors = sb("factors", [P, 3])

        def weight_tiles(js, at):
            for j in js:
                up_hi.append(sb(f"w13_hi{j}", [P, KT, 2, WIDTH[j]], F32R, at))
                up_lo.append(sb(f"w13_lo{j}", [P, KT, 2, WIDTH[j]], F32R, at))
                down_hi.append(sb(f"w2_hi{j}", [P, D], F32R, at))
                down_lo.append(sb(f"w2_lo{j}", [P, D], F32R, at))

        up_hi, up_lo, down_hi, down_lo = [], [], [], []
        weight_tiles(range(EARLY_TILES), ctx)

        with ExitStack() as early:
            mask_sb = sb("mask_sb", [P, KT, D], I32, at=early)
            wa = sb("wa", [P, KT, D], at=early)
            wmod_sb = sb("wmod_sb", [P, KT, 6 * D], at=early)
            lora_raw = sb("lora_raw", [P, LORA_COLS], at=early)
            const = sb("const", [P, CONST_COLS], at=early)
            mask_part = sb("mask_part", [P, KT * NB], at=early)
            block_on = sb("block_on", [P, KT * NB], at=early)
            ct = sb("ct", [P, KT, B], at=early)
            silu_c = sb("silu_c", [P, KT, 1 + B, QUAD], at=early)
            mod_rows = sb("mod_rows", [2 * QUAD, D], at=early)
            bias_raw = sb("bias_raw", [2, D], at=early)
            wa_hi = [sb(f"wa_hi{k}", [P, D], F32R, at=early) for k in range(KT)]
            wa_lo = [sb(f"wa_lo{k}", [P, D], F32R, at=early) for k in range(KT)]
            gates = sb("gates", [P, D], at=early)
            ident = sb("ident", [P, P], at=early)
            bias_parts = sb("bias_parts", [2, D], F32R, at=early)
            ones = sb("ones", [2, P], F32R, at=early)
        weight_tiles(range(EARLY_TILES, HT), ctx)

        acc = [ctx.enter_context(nc.psum_tensor(f"acc{t}", [P, D], F32)) for t in range(T)]
        up_a = ctx.enter_context(nc.psum_tensor("up_a", [P, S], F32))
        up_b = ctx.enter_context(nc.psum_tensor("up_b", [P, S], F32))
        side = [ctx.enter_context(nc.psum_tensor(f"side{n}", [P, 512], F32)) for n in range(2)]

        c_loaded = sem("c_loaded")
        const_loaded = sem("const_loaded")
        ident_loaded = sem("ident_loaded")
        bias_loaded = sem("bias_loaded")
        mask_loaded = sem("mask_loaded")
        lora_loaded = [sem(f"lora_loaded{n}") for n in range(len(LORA_CUTS))]
        silu_c_ready = sem("silu_c_ready")
        bias_high_ready = sem("bias_high_ready")
        bias_ready = sem("bias_ready")
        ones_ready = sem("ones_ready")
        parts_high_ready = sem("parts_high_ready")
        parts_ready = sem("parts_ready")
        mask_summed = sem("mask_summed")
        mask_out = sem("mask_out")
        block_on_ready = sem("block_on_ready")
        wa_masked = sem("wa_masked")
        wa_high_ready = sem("wa_high_ready")
        wa_ready = sem("wa_ready")
        mod_out = sem("mod_out")
        gates_ready = sem("gates_ready")
        cols_ready = sem("cols_ready")
        cols_out = sem("cols_out")
        gate_abs_ready = sem("gate_abs_ready")
        mod_rows_ready = sem("mod_rows_ready")
        silu_c_cleared = sem("silu_c_cleared")
        gate_sign_ready = sem("gate_sign_ready")
        gate_row_ready = sem("gate_row_ready")
        stats_ready = sem("stats_ready")
        moments_ready = sem("moments_ready")
        exponent_ready = sem("exponent_ready")
        variance_ready = sem("variance_ready")
        rstd_ready = sem("rstd_ready")
        normed = sem("normed")
        turned = sem("turned")
        made = {(what, maker): sem(f"{what}_ready_{maker}" if maker else f"{what}_ready")
                for what in MAKER for maker in ["", *sorted(set(MAKER[what].values()))]}
        attn_out = sem("attn_out")
        attn_gated = sem("attn_gated")
        half_on_ready = sem("half_on_ready")
        b13_ready = sem("b13_ready")
        merge_out = sem("merge_out")
        merged = sem("merged")
        w_high_ready = sem("w_high_ready")
        w_ready = sem("w_ready")
        h1_out = sem("h1_out")
        silu_ready = sem("silu_ready")
        h3_out = sem("h3_out")
        g_ready = sem("g_ready")
        g_high_ready = sem("g_high_ready")
        g_low_ready = sem("g_low_ready")
        down_out = sem("down_out")
        down_gated = sem("down_gated")
        rows_added = {(x, maker): sem(f"{x}_ready_{maker}") for x in POOL_ADDS for maker in ("pool", "dve")}
        stored = sem("stored")
        x_loaded = [sem(f"x_loaded{b}") for b in range(B)]
        wmod_a_loaded = [sem(f"wmod_a_loaded{k}") for k in range(KT)]
        wmod_gate_loaded = sem("wmod_gate_loaded")
        wmod_f_loaded = [sem(f"wmod_f_loaded{k}") for k in range(KT)]
        wa_loaded = [sem(f"wa_loaded{k}") for k in range(KT)]
        raw_loaded = [sem(f"raw_loaded{n}") for n in range(SLOTS)]

        side_read = {"mask": block_on_ready, "cols": cols_ready, "attn": attn_gated,
                     "merge": merged}

        def f32(ap):
            return ap.bitcast(F32)

        def weight_parts(r):
            j, n = divmod(r, 3)
            if n < 2:
                half = slice(n * KT // 2, (n + 1) * KT // 2)
                src = raw[:, r % SLOTS, 0:KT * WIDTH[j]].rearrange("p (k m n) -> p k m n", k=KT // 2, m=2)
                return src, up_hi[j][:, half], up_lo[j][:, half]
            return raw[0:WIDTH[j], r % SLOTS], down_hi[j][0:WIDTH[j]], down_lo[j][0:WIDTH[j]]

        def tile_of(n):
            return n // TILES, n % T, n // T % 2

        def done(what, n):
            makers = MAKER[what]
            maker = makers.get(n, "")
            return made[what, maker], sum(makers.get(m, "") == maker for m in range(n + 1))

        def added(x, n):
            by_pool = sum(m in POOL_ADDS[x] for m in range(n + 1))
            if n in POOL_ADDS[x]:
                return rows_added[x, "pool"], by_pool
            return rows_added[x, "dve"], n + 1 - by_pool

        def mod_bank(n):
            return up_b if n == 2 else side[SIDE[("mod", n)] % 2]

        block = ctx.enter_context(nc.Block())

        @block.sync
        def _(sp):
            sp.dma_start(xt[:, 0], x_rows[0]).then_inc(x_loaded[0], 16)
            sp.dma_start(mask_sb[:], mask).then_inc(mask_loaded, 16)
            for k in range(KT):
                sp.dma_start(wmod_sb[:, k, 0:GATE_A * D], wmod_rows[:, k, 0:GATE_A * D]).then_inc(wmod_a_loaded[k], 16)
            gate_cols = slice(GATE_A * D, SHIFT_F * D)
            sp.dma_start(wmod_sb[:, :, gate_cols], wmod_rows[:, :, gate_cols]).then_inc(wmod_gate_loaded, 16)
            for k in range(KT):
                sp.dma_start(wa[:, k], weight[:, k]).then_inc(wa_loaded[k], 16)

            def load_lora(n):
                lo, hi = LORA_CUTS[n]
                sp.dma_start(lora_raw[:, lo:hi], lora[:, lo:hi]).then_inc(lora_loaded[n], 16)

            for n in range(LORA_EARLY):
                load_lora(n)
            for k in range(KT):
                sp.dma_start(wmod_sb[:, k, SHIFT_F * D:], wmod_rows[:, k, SHIFT_F * D:]).then_inc(wmod_f_loaded[k], 16)
            for r in range(3 * HT):
                if r == 3:
                    for n in range(LORA_EARLY, len(LORA_CUTS)):
                        load_lora(n)
                elif r == 5:
                    sp.dma_start(xt[:, 1], x_rows[1]).then_inc(x_loaded[1], 16)
                if r >= SLOTS:
                    sp.wait_ge(w_ready, r - SLOTS + 1)
                sp.dma_start(raw[:, r % SLOTS], ffn[r]).then_inc(raw_loaded[r % SLOTS], 16)
            for n in range(TILES):
                sp.wait_ge(*added("x2", n))
                sp.dma_start(out_rows[n // T, :, n % T], xt[:, n // T, n % T]).then_inc(stored, 16)
            sp.wait_ge(stored, 16 * TILES)

        @block.gpsimd
        def _(pool):
            nc.gpsimd.memset(silu_c[:], 0.0).then_inc(silu_c_cleared, 1)
            nc.gpsimd.memset(factors[:, 0:1], -0.5).then_inc(exponent_ready, 1)
            pool.wait_ge(exponent_ready, 1)

            def root(i):
                pool.wait_ge(moments_ready, i + 1)
                nc.gpsimd.tensor_scalar(var_eps[:, i:i + 1], moments[:, i, 1:2], EPS, None,
                                        ALU.add).then_inc(variance_ready, 1)
                pool.wait_ge(variance_ready, i + 1)
                nc.gpsimd.tensor_tensor(rstd[:, i:i + 1], var_eps[:, i:i + 1], factors[:, 0:1],
                                        ALU.pow).then_inc(rstd_ready, 1)

            def low(n):
                b, t, _ = tile_of(n)
                pool.wait_ge(*done("high", n))
                nc.gpsimd.tensor_tensor(
                    ht_lo[b][:, :, t * P:(t + 1) * P], work[:, n % WORK].rearrange("p (k s) -> p k s", k=KT),
                    f32(ht_hi[b][:, :, t * P:(t + 1) * P]), ALU.subtract).then_inc(made["low", ""], 1)

            def spread(j):
                w = WIDTH[j]
                pool.wait_ge(parts_ready, LORA_EARLY if j < 2 else len(LORA_CUTS))
                pool.wait_ge(half_on_ready, 1)
                if j >= 2:
                    pool.wait_ge(merge_out, 3 * (j - 2) + 2)
                for n in range(2):
                    nc.gpsimd.tensor_scalar(b13[j % 2][:, n, 0:w],
                                            f32(parts[:, LORA_B13 + j * P:LORA_B13 + j * P + w]), factors[:, 1 + n:2 + n],
                                            None, ALU.mult).then_inc(b13_ready, 1)

            def gate_rows(n, roots, lows, spreads):
                pool.wait_ge(gates_ready, n // B + 1)
                pool.wait_ge(rstd_ready, roots)
                pool.wait_ge(made["low", ""], lows)
                if spreads:
                    pool.wait_ge(b13_ready, 2 * spreads)
                if n >= B:
                    pool.wait_ge(attn_gated, T * (n - B + 1))
                nc.gpsimd.partition_broadcast(gate_row[:, n % B], gates[n * QUAD:n * QUAD + 1]
                                              ).then_inc(gate_row_ready, 1)
                pool.wait_ge(gate_row_ready, n + 1)

            def add_rows(x, n, gated):
                b, t = divmod(n, T)
                pool.wait_ge(gated, n + 1)
                nc.gpsimd.tensor_tensor(xt[:, b, t], work[:, t], xt[:, b, t], ALU.add
                                        ).then_inc(rows_added[x, "pool"], 1)

            for i in range(T):
                root(i)
            low(0)
            gate_rows(0, 4, 1, 0)
            add_rows("x1", 0, attn_gated)
            add_rows("x1", 1, attn_gated)
            root(4)
            spread(0)
            root(5)
            add_rows("x1", 2, attn_gated)
            root(6)
            root(7)
            spread(1)
            gate_rows(1, 8, 1, 2)
            low(4)
            low(5)
            gate_rows(2, 8, 3, 2)
            spread(2)
            spread(3)
            root(8)
            root(9)
            spread(4)
            low(8)
            root(10)
            spread(5)
            low(9)
            root(11)
            root(12)
            spread(6)
            low(10)
            root(13)
            spread(7)
            low(11)
            root(14)
            spread(8)
            root(15)
            gate_rows(3, NORMS, 7, 9)
            spread(9)
            low(12)
            low(13)
            spread(10)
            low(14)
            low(15)
            for n in POOL_ADDS["x2"]:
                add_rows("x2", n, down_gated)

        @block.scalar
        def _(act):
            act.dma_start(ident[:], identity).then_inc(ident_loaded, 16)
            act.dma_start(ct[:], c).then_inc(c_loaded, 16)
            act.dma_start(const[:], consts).then_inc(const_loaded, 16)
            act.dma_start(bias_raw[:], bias).then_inc(bias_loaded, 16)
            act.wait_ge(c_loaded, 16)
            act.wait_ge(silu_c_cleared, 1)
            nc.scalar.activation(silu_c[:, :, BOTH, 0:B], ct[:], ACT.Silu).then_inc(silu_c_ready, 1)
            nc.scalar.activation(silu_c[:, :, 1:1 + B, 0], ct[:], ACT.Silu).then_inc(silu_c_ready, 1)
            act.wait_ge(bias_loaded, 16)
            nc.scalar.activation(bias_parts[:], bias_raw[:], ACT.Copy).then_inc(bias_high_ready, 1)

            def modulation(n):
                act.wait_ge(mod_out, 2 * n + 1)
                if n:
                    act.wait_ge(cols_out, n)
                nc.scalar.activation(mod_rows[:], mod_bank(2 * n)[0:2 * QUAD], ACT.Copy
                                     ).then_inc(mod_rows_ready, 1)

            def modulate(i):
                b, t, second = tile_of(i)
                act.wait_ge(turned, i + 1)
                act.wait_ge(cols_ready, second + 1)
                src = side[SIDE[("norm", i)] % 2] if i >= TILES else acc[i % T]
                for k in range(KT):
                    last = nc.scalar.activation(
                        work[:, i % WORK, k * P:(k + 1) * P], src[:, k * P:(k + 1) * P], ACT.Identity,
                        bias=shift[:, second, k, b:b + 1], scale=one_plus[:, second, k, b:b + 1])
                last.then_inc(made["h", ""], 1)

            def high(i):
                b, t, second = tile_of(i)
                act.wait_ge(*done("h", i))
                if second:
                    act.wait_ge(attn_out, T * (b + 1))
                nc.scalar.activation(ht_hi[b][:, :, t * P:(t + 1) * P],
                                     work[:, i % WORK].rearrange("p (k s) -> p k s", k=KT),
                                     ACT.Copy).then_inc(made["high", ""], 1)

            def weight_high(r):
                act.wait_ge(merged, r + 1)
                src, dst, _ = weight_parts(r)
                nc.scalar.activation(dst, src, ACT.Copy).then_inc(w_high_ready, 1)

            def gate_abs(n):
                rows = slice(n * 2 * QUAD, (n + 1) * 2 * QUAD)
                act.wait_ge(mod_out, n + 2)
                nc.scalar.activation(g[rows], mod_bank(n + 1)[rows], ACT.Abs, scale=2.0
                                     ).then_inc(gate_abs_ready, 1)

            def lora_high(n):
                lo, hi = LORA_CUTS[n]
                act.wait_ge(lora_loaded[n], 16)
                nc.scalar.activation(parts[:, lo:hi], lora_raw[:, lo:hi], ACT.Copy).then_inc(parts_high_ready, 1)

            def masked_weight_high(k):
                act.wait_ge(wa_masked, k + 1)
                nc.scalar.activation(wa_hi[k][:], wa[:, k], ACT.Copy).then_inc(wa_high_ready, 1)

            modulation(0)
            modulate(0)
            high(0)
            for k in range(KT):
                masked_weight_high(k)
            gate_abs(0)
            modulate(1)
            high(1)
            lora_high(0)
            modulate(2)
            high(2)
            lora_high(1)
            modulate(3)
            high(3)
            weight_high(0)
            modulation(1)
            gate_abs(1)
            weight_high(1)
            modulate(4)
            high(4)
            modulate(6)
            high(7)
            lora_high(2)
            lora_high(3)
            weight_high(2)
            for s in range(B * HT):
                w = WIDTH[s % HT]
                more = s + 1 < HT
                act.wait_ge(h1_out, s + 1)
                if s:
                    act.wait_ge(g_low_ready, s)
                else:
                    act.wait_ge(gates_ready, 2)
                nc.scalar.activation(g[0:w], up_a[0:w], ACT.Silu).then_inc(silu_ready, 1)
                if more:
                    weight_high(3 * (s + 1))
                    weight_high(3 * (s + 1) + 1)
                act.wait_ge(g_ready, s + 1)
                nc.scalar.activation(g_hi[s % 2][0:w], g[0:w], ACT.Copy).then_inc(g_high_ready, 1)
                if more:
                    weight_high(3 * (s + 1) + 2)
                for n in STEP_TURNS.get(s, ()):
                    modulate(n)
                    high(n)

        @block.vector
        def _(dve):
            def moment(i):
                b, t, second = tile_of(i)
                if second:
                    dve.wait_ge(*added("x1", T * b + t))
                else:
                    dve.wait_ge(x_loaded[b], 16)
                if i >= 2:
                    dve.wait_ge(moments_ready, i - 1)
                nc.vector.bn_stats(stats[:, i % 2], xt[:, b, t]).then_inc(stats_ready, 1)
                dve.wait_ge(stats_ready, i + 1)
                nc.vector.bn_aggr(moments[:, i], stats[:, i % 2]).then_inc(moments_ready, 1)

            def norm(i):
                b, t, _ = tile_of(i)
                dve.wait_ge(rstd_ready, i + 1)
                if i >= WORK:
                    dve.wait_ge(*done("low", i - WORK))
                nc.vector.tensor_scalar(work[:, i % WORK], xt[:, b, t], moments[:, i, 0:1], rstd[:, i:i + 1],
                                        ALU.subtract, ALU.mult).then_inc(normed, 1)

            def modulate(n):
                b, _, second = tile_of(n)
                dve.wait_ge(cols_ready, second + 1)
                dve.wait_ge(turned, n + 1)
                src = side[SIDE[("norm", n)] % 2] if n >= TILES else acc[n % T]
                for k in range(KT):
                    last = nc.vector.tensor_scalar(
                        work[:, n % WORK, k * P:(k + 1) * P], src[:, k * P:(k + 1) * P],
                        one_plus[:, second, k, b:b + 1], shift[:, second, k, b:b + 1], ALU.mult, ALU.add)
                last.then_inc(made["h", "dve"], 1)

            def high(n):
                b, t, second = tile_of(n)
                dve.wait_ge(*done("h", n))
                if second:
                    dve.wait_ge(attn_out, T * (b + 1))
                nc.vector.tensor_copy(ht_hi[b][:, :, t * P:(t + 1) * P],
                                      work[:, n % WORK].rearrange("p (k s) -> p k s", k=KT)
                                      ).then_inc(made["high", "dve"], 1)

            def low(n):
                b, t, _ = tile_of(n)
                dve.wait_ge(*done("high", n))
                nc.vector.tensor_tensor(
                    ht_lo[b][:, :, t * P:(t + 1) * P], work[:, n % WORK].rearrange("p (k s) -> p k s", k=KT),
                    f32(ht_hi[b][:, :, t * P:(t + 1) * P]), ALU.subtract).then_inc(made["low", "dve"], 1)

            def columns(n):
                dve.wait_ge(cols_out, n + 1)
                src = side[SIDE[("cols", n)] % 2][:, 0:KT * 2 * QUAD].rearrange("p (k g b) -> p k g b", k=KT, g=2)
                nc.vector.tensor_copy(shift[:, n], src[:, :, 0, 0:B])
                nc.vector.tensor_scalar(one_plus[:, n], src[:, :, 1, 0:B], 1.0, None, ALU.add
                                        ).then_inc(cols_ready, 1)

            def attn_end(a):
                b, t = divmod(a, T)
                dve.wait_ge(attn_out, a + 1)
                dve.wait_ge(gate_row_ready, b + 1)
                src = side[SIDE[("attn", a)] % 2] if a >= T else acc[a]
                nc.vector.tensor_tensor(work[:, t], src[:], gate_row[:, b], ALU.mult).then_inc(attn_gated, 1)
                if a in POOL_ADDS["x1"]:
                    return
                dve.wait_ge(attn_gated, a + 1)
                nc.vector.tensor_tensor(xt[:, b, t], work[:, t], xt[:, b, t], ALU.add
                                        ).then_inc(rows_added["x1", "dve"], 1)

            def merge(r):
                src, _, _ = weight_parts(r)
                rows = WIDTH[r // 3] if r % 3 == 2 else P
                cols = D if r % 3 == 2 else KT * WIDTH[r // 3]
                dve.wait_ge(raw_loaded[r % SLOTS], 16 * (r // SLOTS + 1))
                dve.wait_ge(merge_out, r + 1)
                w = raw[0:rows, r % SLOTS, 0:cols]
                nc.vector.scalar_tensor_tensor(w, side[SIDE[("merge", r)] % 2][0:rows, 0:cols], SCALING, w,
                                               ALU.mult, ALU.add).then_inc(merged, 1)

            def weight_low(r):
                src, high, low = weight_parts(r)
                dve.wait_ge(w_high_ready, r + 1)
                nc.vector.tensor_tensor(low, src, f32(high), ALU.subtract).then_inc(w_ready, 1)

            def down_end(n):
                b, t = divmod(n, T)
                dve.wait_ge(down_out, n + 1)
                dve.wait_ge(gate_row_ready, B + b + 1)
                if b:
                    dve.wait_ge(*added("x2", n - T))
                nc.vector.tensor_tensor(work[:, t], acc[t][:], gate_row[:, b], ALU.mult).then_inc(down_gated, 1)
                if n in POOL_ADDS["x2"]:
                    return
                dve.wait_ge(down_gated, n + 1)
                nc.vector.tensor_tensor(xt[:, b, t], work[:, t], xt[:, b, t], ALU.add
                                        ).then_inc(rows_added["x2", "dve"], 1)

            moment(0)
            moment(1)
            norm(0)
            moment(2)
            norm(1)
            moment(3)
            norm(2)
            norm(3)
            dve.wait_ge(const_loaded, 16)
            nc.vector.tensor_copy(factors[:, 1:3], const[:, HALF_ON:HALF_ON + 2]).then_inc(half_on_ready, 1)
            nc.vector.tensor_scalar(ones[:], const[0:2, 0:P], 0.0, 1.0, ALU.mult, ALU.add).then_inc(ones_ready, 1)
            dve.wait_ge(bias_high_ready, 1)
            nc.vector.scalar_tensor_tensor(bias_parts[:], f32(bias_parts[:]), const[0:2, KEEP_BIAS:KEEP_BIAS + 1],
                                           bias_raw[:], ALU.mult, ALU.add).then_inc(bias_ready, 1)
            dve.wait_ge(mask_loaded, 16)
            nc.vector.tensor_reduce(mask_part[:], mask_sb[:].rearrange("p k (n c) -> p (k n) c", c=BLOCK),
                                    AX.X, ALU.add).then_inc(mask_summed, 1)
            dve.wait_ge(mask_out, 1)
            nc.vector.tensor_scalar(block_on[:], side[SIDE[("mask", 0)] % 2][:, 0:KT * NB], 0.0, None,
                                    ALU.is_gt).then_inc(block_on_ready, 1)
            columns(0)
            dve.wait_ge(block_on_ready, 1)

            def mask_weight(k):
                dve.wait_ge(wa_loaded[k], 16)
                blocks = wa[:, k].rearrange("p (n c) -> p n c", c=BLOCK)
                nc.vector.tensor_tensor(blocks, blocks,
                                        block_on[:, k * NB:(k + 1) * NB].unsqueeze(2).broadcast_to([P, NB, BLOCK]),
                                        ALU.mult).then_inc(wa_masked, 1)

            for k in range(KT):
                mask_weight(k)
            for k in range(KT):
                dve.wait_ge(wa_high_ready, k + 1)
                nc.vector.tensor_tensor(wa_lo[k][:], wa[:, k], f32(wa_hi[k][:]), ALU.subtract).then_inc(wa_ready, 1)

            def gates_of(n):
                rows = slice(n * 2 * QUAD, (n + 1) * 2 * QUAD)
                dve.wait_ge(gate_abs_ready, n + 1)
                nc.vector.tensor_scalar(gates[rows], mod_bank(n + 1)[rows], 0.0, -0.5,
                                        ALU.is_ge, ALU.add).then_inc(gate_sign_ready, 1)
                dve.wait_ge(gate_sign_ready, n + 1)
                nc.vector.scalar_tensor_tensor(gates[rows], g[rows], 2 * GATE_MIN, gates[rows], ALU.max, ALU.mult
                                               ).then_inc(gates_ready, 1)

            def lora_part(n):
                lo, hi = LORA_CUTS[n]
                keep = KEEP_A if n % 2 else KEEP_B
                dve.wait_ge(parts_high_ready, n + 1)
                nc.vector.scalar_tensor_tensor(parts[:, lo:hi], f32(parts[:, lo:hi]), const[:, keep:keep + 1],
                                               lora_raw[:, lo:hi], ALU.mult, ALU.add).then_inc(parts_ready, 1)

            gates_of(0)
            low(1)
            attn_end(0)
            lora_part(0)
            low(2)
            attn_end(1)
            moment(4)
            lora_part(1)
            low(3)
            norm(4)
            moment(5)
            attn_end(2)
            norm(5)
            attn_end(3)
            moment(6)
            merge(0)
            norm(6)
            moment(7)
            weight_low(0)
            merge(1)
            norm(7)
            columns(1)
            modulate(5)
            high(5)
            modulate(7)
            weight_low(1)
            high(6)
            low(6)
            low(7)
            merge(2)
            gates_of(1)
            for s in range(B * HT):
                w = WIDTH[s % HT]
                more = s + 1 < HT
                if s == STEP_GATES_READ:
                    dve.wait_ge(gate_row_ready, 2 * B)
                if s + 1 <= HT:
                    weight_low(3 * (s + 1) - 1)
                if more:
                    merge(3 * (s + 1))
                    merge(3 * (s + 1) + 1)
                    weight_low(3 * (s + 1))
                    weight_low(3 * (s + 1) + 1)
                dve.wait_ge(silu_ready, s + 1)
                dve.wait_ge(h3_out, s + 1)
                nc.vector.tensor_tensor(g[0:w], up_b[0:w], g[0:w], ALU.mult).then_inc(g_ready, 1)
                if more:
                    merge(3 * (s + 1) + 2)
                dve.wait_ge(g_high_ready, s + 1)
                nc.vector.tensor_tensor(g_lo[s % 2][0:w], g[0:w], f32(g_hi[s % 2][0:w]),
                                        ALU.subtract).then_inc(g_low_ready, 1)
                if s in STEP_ATTN:
                    attn_end(STEP_ATTN[s])
                if s == 0:
                    for n in range(LORA_EARLY, len(LORA_CUTS)):
                        lora_part(n)
                for n in STEP_MOMENTS.get(s, ()):
                    moment(n)
                for n in STEP_TURNS.get(s + 1, ()):
                    norm(n)
                if s == HT:
                    for n in range(T):
                        down_end(n)
            for n in range(T, TILES):
                down_end(n)

        @block.tensor
        def _(pe):
            def free_side(job):
                n = SIDE[job]
                if n >= 2:
                    kind, index = SIDE_JOBS[n - 2]
                    if kind == "norm":
                        pe.wait_ge(*done("h", index))
                    elif kind == "mod":
                        pe.wait_ge(*((gates_ready, 1) if index else (mod_rows_ready, 1)))
                    else:
                        pe.wait_ge(side_read[kind], index + 1)
                return side[n % 2]

            def turn(i):
                dst = free_side(("norm", i)) if i >= TILES else acc[i % T]
                pe.wait_ge(normed, i + 1)
                for k in range(KT):
                    last = nc.tensor.transpose(dst[:, k * P:(k + 1) * P], work[:, i % WORK, k * P:(k + 1) * P],
                                               ident[:])
                last.then_inc(turned, 1)

            def modulation(n):
                dst = up_b if n == 2 else free_side(("mod", n))
                for k in range(KT):
                    if n != 1:
                        pe.wait_ge((wmod_f_loaded if n else wmod_a_loaded)[k], 16)
                    elif k == 0:
                        pe.wait_ge(wmod_gate_loaded, 16)
                    for q, (vector, variant) in enumerate(MOD_PASSES[n]):
                        last = nc.tensor.matmul(dst[q * QUAD:(q + 1) * QUAD], silu_c[:, k, variant],
                                                wmod_sb[:, k, vector * D:(vector + 1) * D],
                                                start=(k == 0), stop=(k == KT - 1))
                last.then_inc(mod_out, 1)

            def columns(n):
                dst = free_side(("cols", n))
                pe.wait_ge(mod_rows_ready, n + 1)
                for k in range(KT):
                    last = nc.tensor.transpose(dst[:, k * 2 * QUAD:(k + 1) * 2 * QUAD],
                                               mod_rows[:, k * P:(k + 1) * P], ident[0:2 * QUAD, 0:2 * QUAD])
                last.then_inc(cols_out, 1)

            def attention(a):
                b, t = divmod(a, T)
                dst = free_side(("attn", a)) if a >= T else acc[a]
                pe.wait_ge(*done("high", TILES * b + t))
                nc.tensor.matmul(dst[:], ones[:], bias_parts[:], start=True, stop=False)
                passes = [(ht_hi, wa_hi), (ht_hi, wa_lo), (ht_lo, wa_hi)]
                for n, (h, wa_part) in enumerate(passes):
                    if n == 2:
                        pe.wait_ge(*done("low", TILES * b + t))
                    for k in range(KT):
                        if a == 0 and n < 2:
                            pe.wait_ge((wa_high_ready, wa_ready)[n], k + 1)
                        last = nc.tensor.matmul(dst[:], h[b][:, k, t * P:(t + 1) * P], wa_part[k][:], start=False,
                                                stop=(n == 2 and k == KT - 1))
                last.then_inc(attn_out, 1)

            def merge(r):
                j, n = divmod(r, 3)
                w = WIDTH[j]
                dst = free_side(("merge", r))
                if n < 2:
                    pe.wait_ge(b13_ready, 2 * (j + 1))
                    for k in range(KT // 2):
                        at = LORA_A13 + (n * KT // 2 + k) * P
                        last = nc.tensor.matmul(dst[:, k * 2 * w:(k + 1) * 2 * w], parts[:, at:at + P],
                                                b13[j % 2][:, :, 0:w], start=True, stop=True)
                else:
                    rows = slice((j % 2) * RANKS, (j % 2 + 1) * RANKS)
                    at = LORA_A2 + (j // 2) * P
                    last = nc.tensor.matmul(dst[0:w], parts[rows, at:at + w], parts[rows, LORA_B2:LORA_B2 + D],
                                            start=True, stop=True)
                last.then_inc(merge_out, 1)

            def up(s, n, dst, signal):
                b, j = divmod(s, HT)
                w = WIDTH[j]
                pe.wait_ge(w_high_ready, 3 * j + 2)
                for m, (weight, h) in enumerate([(up_hi, ht_hi), (up_lo, ht_hi), (up_hi, ht_lo)]):
                    if m == 1:
                        pe.wait_ge(w_ready, 3 * j + 2)
                    elif m == 2 and s == 0:
                        pe.wait_ge(*done("low", 5))
                        pe.wait_ge(*done("low", 7))
                    for k in range(KT):
                        last = nc.tensor.matmul(dst[0:w], weight[j][:, k, n], h[b][:, k],
                                                start=(m == 0 and k == 0), stop=(m == 2 and k == KT - 1))
                last.then_inc(signal, 1)

            def down(s, t):
                b, j = divmod(s, HT)
                w = WIDTH[j]
                pe.wait_ge(g_low_ready, s + 1)
                pe.wait_ge(w_ready, 3 * j + 3)
                if j == 0:
                    pe.wait_ge(*((down_gated, t + 1) if b else (attn_gated, t + 1)))
                hi, lo = (h[s % 2][0:w, t * P:(t + 1) * P] for h in (g_hi, g_lo))
                nc.tensor.matmul(acc[t][:], hi, down_hi[j][0:w], start=(j == 0), stop=False)
                nc.tensor.matmul(acc[t][:], hi, down_lo[j][0:w], start=False, stop=False)
                last = nc.tensor.matmul(acc[t][:], lo, down_hi[j][0:w], start=False, stop=(j == HT - 1))
                if j == HT - 1:
                    last.then_inc(down_out, 1)

            pe.wait_ge(ident_loaded, 16)
            for i in range(T):
                turn(i)
            pe.wait_ge(silu_c_ready, 2)
            modulation(0)
            pe.wait_ge(const_loaded, 16)
            pe.wait_ge(mask_summed, 1)
            nc.tensor.matmul(free_side(("mask", 0))[:, 0:KT * NB], const[:, BLOCK_ONES:BLOCK_ONES + P], mask_part[:],
                             start=True, stop=True).then_inc(mask_out, 1)
            columns(0)
            modulation(1)
            pe.wait_ge(ones_ready, 1)
            pe.wait_ge(bias_ready, 1)
            attention(0)
            attention(1)
            attention(2)
            attention(3)
            pe.wait_ge(parts_ready, LORA_EARLY)
            merge(0)
            merge(1)
            modulation(2)
            turn(4)
            turn(5)
            columns(1)
            turn(6)
            turn(7)
            merge(2)
            for _ in range(WARM_MATMULS):
                nc.tensor.matmul(up_a[:], wa_hi[0][:, 0:P], wa_hi[0][:], start=True, stop=True)
            pe.wait_ge(*done("high", 6))
            pe.wait_ge(*done("high", 7))
            for s in range(B * HT):
                more = s + 1 < HT
                if s == HT:
                    pe.wait_ge(*done("low", NORMS - 1))
                if s:
                    pe.wait_ge(silu_ready, s)
                up(s, 0, up_a, h1_out)
                if more and s != 1:
                    merge(3 * (s + 1))
                    merge(3 * (s + 1) + 1)
                pe.wait_ge(*((g_ready, s) if s else (gates_ready, 2)))
                up(s, 1, up_b, h3_out)
                if s == 1:
                    pe.wait_ge(parts_ready, len(LORA_CUTS))
                    merge(3 * (s + 1))
                    merge(3 * (s + 1) + 1)
                for t in range(T):
                    if s:
                        down(s - 1, t)
                    if t == 1 and more:
                        merge(3 * (s + 1) + 2)
                for n in STEP_TURNS.get(s, ()):
                    turn(n)
                if s in STEP_ATTN:
                    attention(STEP_ATTN[s])
            for t in range(T):
                down(B * HT - 1, t)


def launch_inputs(x, mask, weight, bias, w1, w3, w2, a1, b1, a3, b3, a2, b2, c, wmod):
    def by_feature(m):
        return m.reshape(KT, P, -1).transpose(1, 0, 2)

    ffn = np.zeros((3 * HT, P, D), np.float32)
    for j, w in enumerate(WIDTH):
        both = np.stack([by_feature(up[j * P:j * P + w].T) for up in (w1, w3)], axis=2)
        ffn[3 * j:3 * j + 2, :, 0:KT * w] = both.reshape(P, 2, KT * w).transpose(1, 0, 2)
        ffn[3 * j + 2, 0:w] = w2[:, j * P:j * P + w].T

    def stack(rows):
        return np.tile(rows, (RANKS // R, 1))

    lora = np.zeros((P, LORA_COLS), np.float32)
    for n, (a, b) in enumerate(((a1, b1), (a3, b3))):
        rows = slice(n * RANKS, (n + 1) * RANKS)
        lora[rows, LORA_B13:LORA_B13 + HID] = stack(b.T)
        lora[rows, LORA_A13:LORA_A13 + D] = stack(a)
        lora[rows, LORA_B2:LORA_B2 + D] = stack(b2.T)
    for j, w in enumerate(WIDTH):
        at = LORA_A2 + (j // 2) * P
        lora[(j % 2) * RANKS:(j % 2 + 1) * RANKS, at:at + w] = stack(a2[:, j * P:j * P + w])

    p = np.arange(P)
    consts = np.zeros((P, CONST_COLS), np.float32)
    consts[:, BLOCK_ONES:BLOCK_ONES + P] = p[:, None] // BLOCK == p // BLOCK
    consts[:, KEEP_B] = -(p // (2 * R) % 2)
    consts[:, KEEP_A] = -(p // R % 2)
    consts[:, KEEP_BIAS] = -(p % 2)
    for n in range(2):
        consts[:, HALF_ON + n] = p // RANKS == n
    return {
        "x": x.reshape(B * S, D),
        "mask": by_feature(mask.T),
        "weight": by_feature(weight.T),
        "bias": np.tile(bias, (2, 1)),
        "ffn": ffn,
        "lora": lora,
        "c": by_feature(c.T),
        "wmod": wmod,
        "identity": np.eye(P, dtype=np.float32),
        "consts": consts,
    }


def kernel(L0_attn_data, L0_attn_mask, L0_attn_weight, L0_attn_bias, L0_ffn_w1, L0_ffn_w3, L0_ffn_w2,
           L0_ffn_lora_A1, L0_ffn_lora_B1, L0_ffn_lora_A3, L0_ffn_lora_B3, L0_ffn_lora_A2, L0_ffn_lora_B2,
           L0_c, L0_wmod):
    import concourse.bacc as bacc
    from concourse.bass_utils import run_bass_kernel_spmd

    given = (L0_attn_data, L0_attn_mask, L0_attn_weight, L0_attn_bias, L0_ffn_w1, L0_ffn_w3, L0_ffn_w2,
             L0_ffn_lora_A1, L0_ffn_lora_B1, L0_ffn_lora_A3, L0_ffn_lora_B3, L0_ffn_lora_A2, L0_ffn_lora_B2,
             L0_c, L0_wmod)
    nc = bacc.Bacc("TRN2", target_bir_lowering=False, num_devices=1, dynamic_dma_scratch_size=1024)
    arrays, args = {}, {}
    for name, a in launch_inputs(*(np.asarray(g) for g in given)).items():
        a = np.ascontiguousarray(a)
        arrays[f"in_{name}"] = a
        args[name] = nc.dram_tensor(f"in_{name}", a.shape, mybir.dt.from_np(a.dtype), kind="ExternalInput").ap()
    out = nc.dram_tensor("out", (B, S, D), F32, kind="ExternalOutput").ap()
    build(nc, out=out, **args)
    return run_bass_kernel_spmd(nc, [arrays], core_ids=[0]).results[0]["out"]
```
